# Optimizing a Trainium2 kernel written in Bass

```python
import numpy as np
import jax
import jax.numpy as jnp

def _softmax(x, axis=-1):
    return jax.nn.softmax(x, axis=axis)

def _gelu(x):
    return jax.nn.gelu(x, approximate=True)

def _silu(x):
    return jax.nn.silu(x)

def _sigmoid(x):
    return jax.nn.sigmoid(x)

def _layernorm(x, axis=-1, eps=1e-05):
    m = jnp.mean(x, axis=axis, keepdims=True)
    v = jnp.var(x, axis=axis, keepdims=True)
    return (x - m) / jnp.sqrt(v + eps)

def _scatter_add(tgt, idx, src, axis=0):
    return tgt.at[idx].add(src)

def _segment_sum(src, seg, n):
    return jax.ops.segment_sum(src, seg, n)
kernel_name = 'mk_sandwich_d1_jaxref_r4_a9d572'

def setup_inputs(seed: int=0):
    np.random.seed(seed)
    _w = jnp.asarray

    def _L0_attn_setup():
        import jax, jax.numpy as jnp
        import numpy as np
        B_, L_, D_, N_, R_ = (2, 512, 512, 16, 64)
        DT_MIN, DT_MAX = (0.001, 0.1)
        key = jax.random.key(seed)
        k0, k1, k2, k3 = jax.random.split(key, 4)
        x = jax.random.normal(k0, (B_, L_, D_), jnp.float32)
        W_xproj = jax.random.normal(k1, (R_ + 2 * N_, D_), jnp.float32) * D_ ** (-0.5)
        dt_std = R_ ** (-0.5)
        W_dt = jax.random.uniform(k2, (D_, R_), jnp.float32, -dt_std, dt_std)
        dt = jnp.exp(jax.random.uniform(k3, (D_,), jnp.float32) * (np.log(DT_MAX) - np.log(DT_MIN)) + np.log(DT_MIN))
        b_dt = dt + jnp.log(-jnp.expm1(-dt))
        A_log = jnp.log(jnp.broadcast_to(jnp.arange(1, N_ + 1, dtype=jnp.float32), (D_, N_)))
        D_param = jnp.ones((D_,), jnp.float32)
        return dict(x=x, W_xproj=W_xproj, W_dt=W_dt, b_dt=b_dt, A_log=A_log, D_param=D_param)
    _L0_attn_in = _L0_attn_setup()

    def _L0_ffn_setup():
        import math
        import jax, jax.numpy as jnp
        import numpy as np
        from jax import lax
        D = 512
        I = 256
        E = 32
        K = 4
        NG = 8
        TKG = 3
        NSH = 2
        SCALE = 2.5
        CF = 1.25
        B, S = (2, 512)

        def _router(x, router_w, e_bias):
            scores = jax.nn.sigmoid(x @ router_w.T)
            sc = scores + e_bias[None, :]
            T = x.shape[0]
            gs = sc.reshape(T, NG, E // NG)
            group_scores = lax.top_k(gs, 2)[0].sum(-1)
            _, gidx = lax.top_k(group_scores, TKG)
            gmask = jnp.zeros((T, NG), sc.dtype).at[jnp.arange(T)[:, None], gidx].set(1.0)
            smask = jnp.repeat(gmask, E // NG, axis=1)
            masked = jnp.where(smask > 0, sc, 0.0)
            _, topk_idx = lax.top_k(masked, K)
            topk_w = jnp.take_along_axis(scores, topk_idx, axis=1)
            topk_w = topk_w / (topk_w.sum(-1, keepdims=True) + 1e-20)
            topk_w = topk_w * SCALE
            return (topk_idx.astype(jnp.int32), topk_w)

        def _moe_forward(hidden_states, router_w, e_bias, W_gate, W_up, W_down, shared_gate, shared_up, shared_down):
            b, s, d = hidden_states.shape
            T = b * s
            C = int(math.ceil(CF * T / E))
            EC = E * C
            x = hidden_states.reshape(T, d)
            topk_idx, topk_w = _router(x, router_w, e_bias)
            expert_flat = topk_idx.reshape(-1)
            w_flat = topk_w.reshape(-1)
            tok_flat = jnp.repeat(jnp.arange(T, dtype=jnp.int32), K)
            sort_ix = jnp.argsort(expert_flat)
            e_sorted = expert_flat[sort_ix]
            tok_s = tok_flat[sort_ix]
            w_s = w_flat[sort_ix]
            counts = jnp.zeros(E, jnp.int32).at[e_sorted].add(1)
            group_start = jnp.concatenate([jnp.zeros(1, jnp.int32), jnp.cumsum(counts)[:-1].astype(jnp.int32)])
            pos = jnp.arange(T * K, dtype=jnp.int32) - group_start[e_sorted]
            valid = pos < C
            dest = e_sorted * C + jnp.where(valid, pos, 0)
            slots_token = jnp.zeros(EC, jnp.int32).at[dest].add(jnp.where(valid, tok_s, 0))
            slots_w = jnp.zeros(EC, w_s.dtype).at[dest].add(jnp.where(valid, w_s, 0.0))
            Xp = x[slots_token].reshape(E, C, d)
            G = jnp.einsum('ecd,edi->eci', Xp, W_gate)
            U = jnp.einsum('ecd,edi->eci', Xp, W_up)
            Y = jnp.einsum('eci,eid->ecd', jax.nn.silu(G) * U, W_down)
            Yf = Y.reshape(EC, d) * slots_w[:, None]
            out = jnp.zeros((T, d), x.dtype).at[slots_token].add(Yf)
            shared = jax.nn.silu(x @ shared_gate.T) * (x @ shared_up.T) @ shared_down.T
            return (out + shared).reshape(b, s, d)
        key = jax.random.key(seed)
        ks = jax.random.split(key, 8)

        def rn(k, shape, scale=0.02):
            return jax.random.normal(k, shape, jnp.float32) * scale
        return {'hidden_states': jax.random.normal(ks[0], (B, S, D), jnp.float32), 'router_w': rn(ks[1], (E, D)), 'e_bias': jnp.zeros((E,), jnp.float32), 'W_gate': rn(ks[2], (E, D, I)), 'W_up': rn(ks[3], (E, D, I)), 'W_down': rn(ks[4], (E, I, D)), 'shared_gate': rn(ks[5], (I * NSH, D)), 'shared_up': rn(ks[6], (I * NSH, D)), 'shared_down': rn(ks[7], (D, I * NSH))}
    _L0_ffn_in = _L0_ffn_setup()
    _d = {'L0_attn_x': _L0_attn_in['x'], 'L0_attn_W_xproj': _L0_attn_in['W_xproj'], 'L0_attn_W_dt': _L0_attn_in['W_dt'], 'L0_attn_b_dt': _L0_attn_in['b_dt'], 'L0_attn_A_log': _L0_attn_in['A_log'], 'L0_attn_D_param': _L0_attn_in['D_param'], 'L0_ffn_router_w': _L0_ffn_in['router_w'], 'L0_ffn_e_bias': _L0_ffn_in['e_bias'], 'L0_ffn_W_gate': _L0_ffn_in['W_gate'], 'L0_ffn_W_up': _L0_ffn_in['W_up'], 'L0_ffn_W_down': _L0_ffn_in['W_down'], 'L0_ffn_shared_gate': _L0_ffn_in['shared_gate'], 'L0_ffn_shared_up': _L0_ffn_in['shared_up'], 'L0_ffn_shared_down': _L0_ffn_in['shared_down']}
    _x0 = _d['L0_attn_x']
    _d['L0_attn_x'] = jax.random.normal(jax.random.fold_in(jax.random.key(seed), 1), (4, 512, 512), dtype=_x0.dtype)
    del _x0
    return _d

def reference(L0_attn_x, L0_attn_W_xproj, L0_attn_W_dt, L0_attn_b_dt, L0_attn_A_log, L0_attn_D_param, L0_ffn_router_w, L0_ffn_e_bias, L0_ffn_W_gate, L0_ffn_W_up, L0_ffn_W_down, L0_ffn_shared_gate, L0_ffn_shared_up, L0_ffn_shared_down):

    def _L0_attn_ref(x, W_xproj, W_dt, b_dt, A_log, D_param):
        import jax, jax.numpy as jnp
        import numpy as np
        B_, L_, D_, N_, R_ = (2, 512, 512, 16, 64)
        DT_MIN, DT_MAX = (0.001, 0.1)
        R = W_dt.shape[1]
        N = A_log.shape[1]
        x_dbl = jnp.einsum('bld,ed->ble', x, W_xproj)
        delta_raw, Bm, Cm = jnp.split(x_dbl, [R, R + N], axis=-1)
        delta = jax.nn.softplus(jnp.einsum('blr,dr->bld', delta_raw, W_dt) + b_dt)
        A = -jnp.exp(A_log)
        dA = jnp.exp(jnp.einsum('bld,dn->bldn', delta, A))
        dBx = jnp.einsum('bld,bln->bldn', delta * x, Bm)

        def step(h, inp):
            dA_t, dBx_t, C_t = inp
            h = dA_t * h + dBx_t
            y_t = jnp.einsum('bdn,bn->bd', h, C_t)
            return (h, y_t)
        h0 = jnp.zeros((x.shape[0], x.shape[2], N), x.dtype)
        xs = (jnp.moveaxis(dA, 1, 0), jnp.moveaxis(dBx, 1, 0), jnp.moveaxis(Cm, 1, 0))
        _, ys = jax.lax.scan(step, h0, xs)
        y = jnp.moveaxis(ys, 0, 1)
        return y + x * D_param

    def _L0_ffn_ref(hidden_states, router_w, e_bias, W_gate, W_up, W_down, shared_gate, shared_up, shared_down):
        import math
        import jax, jax.numpy as jnp
        import numpy as np
        from jax import lax
        D = 512
        I = 256
        E = 32
        K = 4
        NG = 8
        TKG = 3
        NSH = 2
        SCALE = 2.5
        CF = 1.25
        B, S = (2, 512)

        def _router(x, router_w, e_bias):
            scores = jax.nn.sigmoid(x @ router_w.T)
            sc = scores + e_bias[None, :]
            T = x.shape[0]
            gs = sc.reshape(T, NG, E // NG)
            group_scores = lax.top_k(gs, 2)[0].sum(-1)
            _, gidx = lax.top_k(group_scores, TKG)
            gmask = jnp.zeros((T, NG), sc.dtype).at[jnp.arange(T)[:, None], gidx].set(1.0)
            smask = jnp.repeat(gmask, E // NG, axis=1)
            masked = jnp.where(smask > 0, sc, 0.0)
            _, topk_idx = lax.top_k(masked, K)
            topk_w = jnp.take_along_axis(scores, topk_idx, axis=1)
            topk_w = topk_w / (topk_w.sum(-1, keepdims=True) + 1e-20)
            topk_w = topk_w * SCALE
            return (topk_idx.astype(jnp.int32), topk_w)

        def _moe_forward(hidden_states, router_w, e_bias, W_gate, W_up, W_down, shared_gate, shared_up, shared_down):
            b, s, d = hidden_states.shape
            T = b * s
            C = int(math.ceil(CF * T / E))
            EC = E * C
            x = hidden_states.reshape(T, d)
            topk_idx, topk_w = _router(x, router_w, e_bias)
            expert_flat = topk_idx.reshape(-1)
            w_flat = topk_w.reshape(-1)
            tok_flat = jnp.repeat(jnp.arange(T, dtype=jnp.int32), K)
            sort_ix = jnp.argsort(expert_flat)
            e_sorted = expert_flat[sort_ix]
            tok_s = tok_flat[sort_ix]
            w_s = w_flat[sort_ix]
            counts = jnp.zeros(E, jnp.int32).at[e_sorted].add(1)
            group_start = jnp.concatenate([jnp.zeros(1, jnp.int32), jnp.cumsum(counts)[:-1].astype(jnp.int32)])
            pos = jnp.arange(T * K, dtype=jnp.int32) - group_start[e_sorted]
            valid = pos < C
            dest = e_sorted * C + jnp.where(valid, pos, 0)
            slots_token = jnp.zeros(EC, jnp.int32).at[dest].add(jnp.where(valid, tok_s, 0))
            slots_w = jnp.zeros(EC, w_s.dtype).at[dest].add(jnp.where(valid, w_s, 0.0))
            Xp = x[slots_token].reshape(E, C, d)
            G = jnp.einsum('ecd,edi->eci', Xp, W_gate)
            U = jnp.einsum('ecd,edi->eci', Xp, W_up)
            Y = jnp.einsum('eci,eid->ecd', jax.nn.silu(G) * U, W_down)
            Yf = Y.reshape(EC, d) * slots_w[:, None]
            out = jnp.zeros((T, d), x.dtype).at[slots_token].add(Yf)
            shared = jax.nn.silu(x @ shared_gate.T) * (x @ shared_up.T) @ shared_down.T
            return (out + shared).reshape(b, s, d)
        return _moe_forward(hidden_states, router_w, e_bias, W_gate, W_up, W_down, shared_gate, shared_up, shared_down)
    x = L0_attn_x
    x = x + _layernorm(_L0_attn_ref(_layernorm(x, axis=-1), L0_attn_W_xproj, L0_attn_W_dt, L0_attn_b_dt, L0_attn_A_log, L0_attn_D_param), axis=-1)
    x = x + _layernorm(_L0_ffn_ref(_layernorm(x, axis=-1), L0_ffn_router_w, L0_ffn_e_bias, L0_ffn_W_gate, L0_ffn_W_up, L0_ffn_W_down, L0_ffn_shared_gate, L0_ffn_shared_up, L0_ffn_shared_down), axis=-1)
    return x

_drawn_inputs = setup_inputs


def setup_inputs(seed=0):
    import zlib

    import numpy as np

    out = dict(_drawn_inputs(seed))
    spreads = {'L0_attn_D_param': (1.0, 0.2), 'L0_ffn_e_bias': (0.0, 0.1)}
    factors = {}
    for name, (base, spread) in spreads.items():
        noise = np.random.default_rng([zlib.crc32(name.encode()), seed]).standard_normal(out[name].shape)
        drawn = base * np.exp(spread * noise) if base else spread * noise
        out[name] = jnp.asarray(drawn.astype(out[name].dtype))
    for name, factor in factors.items():
        out[name] = (out[name] * factor).astype(out[name].dtype)
    return out
```

```python
from contextlib import ExitStack

import concourse.bass as bass
from concourse import mybir

F32 = mybir.dt.float32
I32 = mybir.dt.int32
U32 = mybir.dt.uint32
ACT = mybir.ActivationFunctionType
ALU = mybir.AluOpType
AX_X = mybir.AxisListType.X

P = 128
B, L, D = 4, 512, 512
T = B * L
TT = L // P
DT = D // P
N = 16
R = 64
XE = R + 2 * N
E, K = 32, 4
NG, TKG = 8, 3
EG = E // NG
I = 256
IT = I // P
IS = 512
ST = IS // P
CAP = -(-T * 5 // (4 * E))
CAPW = 96
SLOTS = E * CAP
SCALE = 2.5
EPS = 1e-5
WE = DT * I * 2 + IT * D
WBUF = 4
DA_RING = 6
BIG = 1.0e6


POST_STEPS = {
    3: [("x2T", 0), ("x2T", 1), ("x2T", 2), ("x2T", 3)],
    4: [("lg", 0), ("g", 0)],
    5: [("sc", 0), ("u", 0)],
    6: [("g", 1)],
    7: [("mT", 0), ("u", 1)],
    8: [("g", 2), ("u", 2)],
    9: [("pos", 0), ("g", 3), ("u", 3)],
    10: [("dn", 0)],
    11: [("dn", 1), ("dn", 2)],
    12: [("dn", 3)],
}
FRONT_STEPS = {
    10: [("xnT", 0), ("xnT", 1), ("xnT", 2), ("xnT", 3)],
    11: [("xdbl", 0), ("bc", 0)],
    12: [("draw", 0), ("draw", 1)],
    13: [("draw", 2), ("draw", 3)],
    15: [("dxt", 0), ("dxt", 1), ("dxt", 2), ("dxt", 3)],
}


def misc_order():
    def part(steps, n, b):
        return [(name, b, i) for name, i in steps.get(n, [])]
    order = [u for n in range(N) for u in part(FRONT_STEPS, n, 0)]
    for b in range(B):
        for n in range(N):
            if b > 0:
                order += part(POST_STEPS, n, b - 1)
            if b + 1 < B:
                order += part(FRONT_STEPS, n, b + 1)
    return order + [u for n in range(N) for u in part(POST_STEPS, n, B - 1)]


MISC = {u: (i % 2, i // 2) for i, u in enumerate(misc_order())}


def norm_order():
    order = [("x", 0)]
    for b in range(B):
        if b > 0:
            order += [("y", b - 1), ("x1", b - 1)]
        if b + 1 < B:
            order += [("x", b + 1)]
    return order + [("y", B - 1), ("x1", B - 1)] + [("sum", b) for b in range(B)]


NORM = {u: i for i, u in enumerate(norm_order())}
PLACE = {"x": 0, "y": 1, "x1": 2, "sum": 3}


def sandwich(nc, x, wxT, wdT, b_dt, A_log, Dp, rwT, e_bias, wexp, sgT, suT, sdT, out):
    with ExitStack() as ctx:
        def sb(name, shape, dt=F32):
            return ctx.enter_context(nc.sbuf_tensor(name, shape, dt))

        def sem(name):
            return ctx.enter_context(nc.semaphore(name))

        x2_rows = nc.dram_tensor("x2_rows", [T + CAP, D], F32).ap()
        ffn_rows = nc.dram_tensor("ffn_rows", [T + CAP, D], F32).ap()
        slot_table = nc.dram_tensor("slot_table", [SLOTS, 2], I32).ap()

        arena = sb("arena", [P, 6 * TT * D + DA_RING * L + 2 * DT * L])
        used = [0]

        def cut(n):
            used[0] += n
            return arena[:, used[0] - n:used[0]]
        delta, dx = [None, None], [None, None]
        for k in range(2):
            delta[k] = cut(DT * L).rearrange("p (a l) -> p a l", a=DT)
            dx[k] = cut(TT * D).rearrange("p (a l) -> p a l", a=TT)
        dxs = cut(2 * TT * D).rearrange("p (s a l) -> p s a l", s=2, a=TT)
        dA = cut(DA_RING * L).rearrange("p (s l) -> p s l", s=DA_RING)
        h = cut(2 * DT * L).rearrange("p (s a l) -> p s a l", s=2, a=DT)
        wring = [arena[:, k * WE:(k + 1) * WE] for k in range(WBUF)]
        used[0] = WBUF * WE
        xg = [cut(D) for _ in range(4)]
        xgT = [cut(DT * CAPW).rearrange("p (a c) -> p a c", a=DT) for _ in range(2)]
        sg = [cut(IT * CAPW).rearrange("p (a c) -> p a c", a=IT) for _ in range(2)]
        hid = [cut(IT * CAPW).rearrange("p (a c) -> p a c", a=IT) for _ in range(2)]
        ye = [cut(D) for _ in range(2)]
        assert used[0] <= arena.shape[1]
        fin = [arena[:, k * TT * D:(k + 1) * TT * D].rearrange("p (a l) -> p a l", a=TT) for k in range(B)]

        xall = sb("xall", [P, B, TT, D])
        y = sb("y", [P, 2, TT, D])
        nrm = sb("nrm", [P, TT, D])
        tr = sb("tr", [P, DT, L])
        xdbl = sb("xdbl", [XE, L])
        bct = sb("bct", [P, 2, TT, XE])
        hs = sb("hs", [P, ST, L])
        soft = hs
        onep = sb("onep", [P, 2, L])
        shout = sb("shout", [P, 2, D])
        wx, wd, rw = sb("wx", [P, DT, XE]), sb("wd", [R, D]), sb("rw", [P, DT, E])
        wsg, wsu, wsd = sb("wsg", [P, DT, IS]), sb("wsu", [P, DT, IS]), sb("wsd", [P, ST, D])
        dbc, ebias = sb("dbc", [P, D]), sb("ebias", [P, E])
        bdt, nA = sb("bdt", [P, DT]), sb("nA", [P, DT, N])
        ident, mhalf = sb("ident", [P, P]), sb("mhalf", [P, TT])
        iota_e, tok, ones = sb("iota_e", [P, E]), sb("tok", [P, B * TT], I32), sb("ones", [E, L])
        stat, mv = sb("stat", [P, 4, TT, 6]), sb("mv", [P, 4, TT, 2])
        vpe, rstd = sb("vpe", [P, 4, TT]), sb("rstd", [P, 4, TT])
        lgT, score, scb = sb("lgT", [E, L]), sb("score", [P, TT, E]), sb("scb", [P, TT, E])
        pair, gs = sb("pair", [P, 5, TT * NG]), sb("gs", [P, TT * NG])
        top8, top8i, topf = sb("top8", [P, TT, 8]), sb("top8i", [P, TT, 8], U32), sb("topf", [P, TT, 8])
        geq, gmask = sb("geq", [P, TT, TKG, NG]), sb("gmask", [P, TT, NG])
        onehot, picked = sb("onehot", [P, TT, K, E]), sb("picked", [P, TT, K, E])
        mask, count, carry = sb("mask", [P, TT, E]), sb("count", [E, L]), sb("carry", [E, 1])
        wsel, wsum = sb("wsel", [P, TT, K]), sb("wsum", [P, TT])
        possel, over, dest = sb("possel", [P, TT, K]), sb("over", [P, TT, K]), sb("dest", [P, TT, K])
        desti = sb("desti", [P, 2, TT * K], I32)
        entry = sb("entry", [P, 2, TT, K, 2], I32)
        slots = sb("slots", [CAP, E, 2], I32)

        def bank(name):
            return ctx.enter_context(nc.psum_tensor(name, [P, 512], F32))[:, :]
        ps_dbx = [bank(f"ps_dbx{i}") for i in range(DT)]
        ps_ht = [bank(f"ps_ht{i}") for i in range(2)]
        ps_misc = [bank(f"ps_misc{i}") for i in range(2)]
        ps_xg, ps_gu, ps_y = ps_dbx[0:2], ps_dbx[2:4], ps_ht

        x_loaded = [sem(f"x_loaded{b}") for b in range(B)]
        small_loaded, shared_loaded = sem("small_loaded"), sem("shared_loaded")
        pool_const, dve_const = sem("pool_const"), sem("dve_const")
        nA_exp, nA_ready = sem("nA_exp"), sem("nA_ready")
        dA_ready, dxs_ready, dbx_ready = sem("dA_ready"), sem("dxs_ready"), sem("dbx_ready")
        h_ready, ht_ready, y_added = sem("h_ready"), sem("ht_ready"), sem("y_added")
        misc_full = [sem("misc_full0"), sem("misc_full1")]
        misc_taken = [sem("misc_taken0"), sem("misc_taken1")]
        dve_seq, pool_seq = sem("dve_seq"), sem("pool_seq")
        var_ready, rstd_ready = sem("var_ready"), sem("rstd_ready")
        xn_ready, y_init = sem("xn_ready"), sem("y_init")
        abs_ready, exp_ready, onep_ready = sem("abs_ready"), sem("exp_ready"), sem("onep_ready")
        corr_ready, ln_ready = sem("corr_ready"), sem("ln_ready")
        log1p_ready, delta_ready, dxT_ready = sem("log1p_ready"), sem("delta_ready"), sem("dxT_ready")
        yn_ready, x1_ready, x2_ready = sem("yn_ready"), sem("x1_ready"), sem("x2_ready")
        x2_stored = sem("x2_stored")
        mask_ready, dest_ready = sem("mask_ready"), sem("dest_ready")
        tanh_ready = sem("tanh_ready")
        shared_stored = [sem("shared_stored0"), sem("shared_stored1")]
        filled = sem("filled")
        slots_written = [sem("slots_written0"), sem("slots_written1")]
        slots_loaded = sem("slots_loaded")
        w_loaded = [sem(f"w_loaded{k}") for k in range(WBUF)]
        gathered = [sem(f"gathered{k}") for k in range(4)]
        xg_turned, silu_ready, pad_ready = sem("xg_turned"), sem("silu_ready"), sem("pad_ready")
        xgT_ready, gu_ready, hid_ready = sem("xgT_ready"), sem("gu_ready"), sem("hid_ready")
        y_ready, ye_ready, added = sem("y_ready"), sem("ye_ready"), sem("added")
        fin_loaded = [sem(f"fin_loaded{b}") for b in range(B)]
        fin_normed, fin_ready, fin_stored = sem("fin_normed"), sem("fin_ready"), sem("fin_stored")

        def wait_full(eng, *u):
            k, turn = MISC[u]
            eng.wait_ge(misc_full[k], turn + 1)
            return ps_misc[k]

        def wait_taken(eng, *u):
            k, turn = MISC[u]
            eng.wait_ge(misc_taken[k], turn + 1)

        def taken(*u):
            return misc_taken[MISC[u][0]]

        def fronts(b):
            return min(b + 2, B)

        block = ctx.enter_context(nc.Block())

        @block.sync
        def _(sp):
            xv = x.rearrange("b (t p) d -> b p t d", p=P)
            sp.dma_start(xall[:, 0], xv[0]).then_inc(x_loaded[0], 16)
            sp.dma_start(wx[:], wxT.rearrange("(t p) e -> p t e", p=P)).then_inc(small_loaded, 16)
            sp.dma_start(wd[:], wdT).then_inc(small_loaded, 16)
            sp.dma_start(bdt[:], b_dt).then_inc(small_loaded, 16)
            sp.dma_start(nA[:], A_log.rearrange("(t p) n -> p t n", p=P)).then_inc(small_loaded, 16)
            sp.dma_start(dbc[:], Dp.partition_broadcast(P)).then_inc(small_loaded, 16)
            sp.dma_start(rw[:], rwT.rearrange("(t p) e -> p t e", p=P)).then_inc(small_loaded, 16)
            sp.dma_start(ebias[:], e_bias.partition_broadcast(P)).then_inc(small_loaded, 16)
            sp.dma_start(xall[:, 1], xv[1]).then_inc(x_loaded[1], 16)
            sp.dma_start(wsg[:], sgT.rearrange("(t p) i -> p t i", p=P)).then_inc(shared_loaded, 16)
            sp.dma_start(wsu[:], suT.rearrange("(t p) i -> p t i", p=P)).then_inc(shared_loaded, 16)
            sp.dma_start(wsd[:], sdT.rearrange("(t p) d -> p t d", p=P)).then_inc(shared_loaded, 16)
            for b in range(2, B):
                sp.dma_start(xall[:, b], xv[b]).then_inc(x_loaded[b], 16)
            sp.wait_ge(dve_const, 2)
            sp.wait_ge(pool_const, 4)
            sp.dma_start(x2_rows[T:T + CAP, :], y[0:CAP, 1, 0, :]).then_inc(filled, 16)
            sp.dma_start(ffn_rows[T:T + CAP, :], y[0:CAP, 1, 0, :]).then_inc(filled, 16)
            sp.dma_start(slot_table.rearrange("(e c) k -> c e k", c=CAP), slots[:]).then_inc(filled, 16)
            for b in range(B):
                if b == B - 1:
                    sp.wait_ge(y_added, 4 * N * B)
                    for k in range(1, WBUF):
                        sp.dma_start(wring[k], wexp[k]).then_inc(w_loaded[k], 16)
                rows = x2_rows[b * L:(b + 1) * L, :].rearrange("(t p) d -> p t d", p=P)
                sp.wait_ge(x2_ready, 4 * (b + 1))
                sp.dma_start(rows, nrm[:]).then_inc(x2_stored, 16)
                for tt in range(TT):
                    k = b * TT + tt
                    wait_taken(sp, "dn", b, tt)
                    sp.dma_start(ffn_rows[k * P:(k + 1) * P, :], shout[:, k % 2]).then_inc(shared_stored[k % 2], 16)
                if b == B - 2:
                    sp.wait_ge(dA_ready, 4 * N * (B - 1))
                    sp.wait_ge(dxs_ready, 4 * N * (B - 1))
                    sp.dma_start(wring[0], wexp[0]).then_inc(w_loaded[0], 16)
            for k in range(2):
                sp.wait_ge(slots_written[k], 16 * TT * K * B // 2)
            sp.dma_start(slots[:], slot_table.rearrange("(e c) k -> c e k", c=CAP)).then_inc(slots_loaded, 16)
            with sp.Fori(1, E // WBUF) as q:
                for k in range(WBUF):
                    sp.wait_ge(y_ready, q * WBUF + (k - WBUF + 3))
                    sp.dma_start(wring[k], wexp[bass.ds(q * WBUF + k, 1)].rearrange("a p w -> (a p) w")).then_inc(w_loaded[k], 16)
            sp.wait_ge(added, 16 * E)
            for b in range(B):
                rows = ffn_rows[b * L:(b + 1) * L, :].rearrange("(t p) d -> p t d", p=P)
                sp.dma_start(fin[b], rows).then_inc(fin_loaded[b], 16)
            ov = out.rearrange("b (t p) d -> b p t d", p=P)
            for b in range(B):
                sp.wait_ge(fin_ready, 4 * (b + 1))
                sp.dma_start(ov[b], fin[b]).then_inc(fin_stored, 16)
            sp.wait_ge(fin_stored, 16 * B)

        @block.tensor
        def _(pe):
            def turn4(dst, full, src, width=P):
                for j in range(4):
                    k = src(j).shape[0]
                    last = nc.tensor.transpose(dst[0:src(j).shape[1], j * width:j * width + k], src(j), ident[0:k, 0:k])
                last.then_inc(full, 1)

            def product(dst, full, w, v, k_tiles=4):
                for k in range(k_tiles):
                    last = nc.tensor.matmul(dst, w(k), v(k), start=(k == 0), stop=(k == k_tiles - 1))
                last.then_inc(full, 1)

            def misc(name, b, i):
                k, turn = MISC[name, b, i]
                if turn > 0:
                    pe.wait_ge(misc_taken[k], turn)
                ps, full = ps_misc[k], misc_full[k]
                if name == "xnT":
                    pe.wait_ge(xn_ready, 4 * (b + 1))
                    turn4(ps, full, lambda tt: nrm[:, tt, i * P:(i + 1) * P])
                elif name == "xdbl":
                    pe.wait_ge(small_loaded, 16 * 7)
                    for j in range(DT):
                        wait_taken(pe, "xnT", b, j)
                    product(ps[0:XE, :], full, lambda k: wx[:, k, :], lambda k: tr[:, k, :])
                elif name == "bc":
                    wait_taken(pe, "xdbl", b, 0)
                    for tt in range(TT):
                        last = nc.tensor.transpose(ps[:, tt * XE:(tt + 1) * XE], xdbl[:, tt * P:(tt + 1) * P], ident[0:XE, 0:XE])
                    last.then_inc(full, 1)
                elif name == "draw":
                    wait_taken(pe, "xdbl", b, 0)
                    product(ps[:, :], full, lambda k: wd[:, i * P:(i + 1) * P], lambda k: xdbl[0:R, :], 1)
                elif name == "dxt":
                    pe.wait_ge(dxT_ready, 4 * (b + 1))
                    turn4(ps, full, lambda dt: soft[:, dt, i * P:(i + 1) * P])
                elif name == "x2T":
                    pe.wait_ge(x2_ready, 4 * (b + 1))
                    turn4(ps, full, lambda tt: nrm[:, tt, i * P:(i + 1) * P])
                elif name == "lg":
                    for j in range(DT):
                        wait_taken(pe, "x2T", b, j)
                    product(ps[0:E, :], full, lambda k: rw[:, k, :], lambda k: tr[:, k, :])
                elif name == "sc":
                    wait_taken(pe, "lg", b, 0)
                    for tt in range(TT):
                        last = nc.tensor.transpose(ps[:, tt * E:(tt + 1) * E], lgT[:, tt * P:(tt + 1) * P], ident[0:E, 0:E])
                    last.then_inc(full, 1)
                elif name in ("g", "u"):
                    pe.wait_ge(shared_loaded, 16 * 3)
                    w = wsg if name == "g" else wsu
                    product(ps[:, :], full, lambda k: w[:, k, i * P:(i + 1) * P], lambda k: tr[:, k, :])
                elif name == "mT":
                    pe.wait_ge(mask_ready, b + 1)
                    for tt in range(TT):
                        last = nc.tensor.transpose(ps[0:E, tt * P:(tt + 1) * P], mask[:, tt, :], ident[:, :])
                    last.then_inc(full, 1)
                elif name == "pos":
                    wait_taken(pe, "mT", b, 0)
                    for tt in range(TT):
                        last = nc.tensor.transpose(ps[:, tt * E:(tt + 1) * E], count[:, tt * P:(tt + 1) * P], ident[0:E, 0:E])
                    last.then_inc(full, 1)
                elif name == "dn":
                    for j in range(ST):
                        wait_taken(pe, "u", b, j)
                    product(ps[:, :], full, lambda k: hs[:, k, i * P:(i + 1) * P], lambda k: wsd[:, k, :])

            def turn_dbx(s, dt):
                u = 4 * s + dt
                pe.wait_ge(dxs_ready, 4 * (s + 1))
                if s >= 1:
                    pe.wait_ge(h_ready, u - 3)
                turn4(ps_dbx[dt], dbx_ready, lambda tt: dxs[:, s % 2, tt, dt * P:(dt + 1) * P])

            def turn_h(s, tt):
                u = 4 * s + tt
                pe.wait_ge(h_ready, 4 * (s + 1))
                if u >= 2:
                    pe.wait_ge(y_added, u - 1)
                turn4(ps_ht[u % 2], ht_ready, lambda dt: h[:, s % 2, dt, tt * P:(tt + 1) * P])

            pe.wait_ge(pool_const, 2)
            for n in range(N):
                for name, i in FRONT_STEPS.get(n, []):
                    misc(name, 0, i)
            for b in range(B):
                for n in range(N):
                    s = b * N + n
                    for j in range(4):
                        turn_dbx(s, j)
                        if s >= 1:
                            turn_h(s - 1, j)
                    for name, i in POST_STEPS.get(n, []) if b > 0 else []:
                        misc(name, b - 1, i)
                    for name, i in FRONT_STEPS.get(n, []) if b + 1 < B else []:
                        misc(name, b + 1, i)
            for j in range(4):
                turn_h(B * N - 1, j)
            for n in range(N):
                for name, i in POST_STEPS.get(n, []):
                    misc(name, B - 1, i)

            def turn_xg(q, r):
                pe.wait_ge(gathered[r % 4], (q + r // 4 + 1) * 16)
                pe.wait_ge(xgT_ready, q * 4 + (r + 1))
                for k in range(DT):
                    last = nc.tensor.transpose(ps_xg[r % 2][:, k * CAP:(k + 1) * CAP],
                                               xg[r % 4][0:CAP, k * P:(k + 1) * P], ident[0:CAP, 0:CAP])
                last.then_inc(xg_turned, 1)

            def gate_up(q, r):
                w = wring[r % WBUF][:, 0:2 * DT * I].rearrange("p (m k i) -> p m k i", m=2, k=DT)
                pe.wait_ge(w_loaded[r % WBUF], (q + r // WBUF + 1) * 16)
                pe.wait_ge(xgT_ready, q * 4 + (r + 3))
                pe.wait_ge(hid_ready, q * 4 + (r + 1))
                for m in range(2):
                    for it in range(IT):
                        c = (m * IT + it) * CAPW
                        for k in range(DT):
                            last = nc.tensor.matmul(ps_gu[r % 2][:, c:c + CAPW], w[:, m, k, it * P:(it + 1) * P],
                                                    xgT[r % 2][:, k, :], start=(k == 0), stop=(k == DT - 1))
                last.then_inc(gu_ready, 1)

            def down(q, r):
                w = wring[r % WBUF][:, 2 * DT * I:].rearrange("p (k d) -> p k d", k=IT)
                pe.wait_ge(hid_ready, q * 4 + (r + 3))
                pe.wait_ge(ye_ready, q * 4 + (r + 1))
                for k in range(IT):
                    last = nc.tensor.matmul(ps_y[r % 2][0:CAP, :], hid[r % 2][:, k, 0:CAP], w[:, k, :],
                                            start=(k == 0), stop=(k == IT - 1))
                last.then_inc(y_ready, 1)

            pe.sem_inc(gu_ready, 2)
            pe.sem_inc(y_ready, 2)
            pe.wait_ge(pad_ready, 2)
            turn_xg(0, 0)
            turn_xg(0, 1)
            gate_up(0, 0)
            with pe.Fori(0, E // 4 - 1) as q:
                for r in range(4):
                    turn_xg(q, r + 2)
                    gate_up(q, r + 1)
                    down(q, r)
            for r in range(4):
                if r + 2 < 4:
                    turn_xg(E // 4 - 1, r + 2)
                if r + 1 < 4:
                    gate_up(E // 4 - 1, r + 1)
                down(E // 4 - 1, r)

        @block.scalar
        def _(act):
            def take(u, dst, src, func=ACT.Copy, **kw):
                wait_full(act, *u)
                nc.scalar.activation(dst, src, func, **kw).then_inc(taken(*u), 1)

            def exps(s):
                b, n = divmod(s, N)
                if n == 0:
                    act.wait_ge(delta_ready, 4 * (b + 1))
                    act.wait_ge(nA_ready, 1)
                for dt in range(DT):
                    u = 4 * s + dt
                    if u >= DA_RING:
                        act.wait_ge(h_ready, u - DA_RING + 1)
                    nc.scalar.activation(dA[:, u % DA_RING], delta[b % 2][:, dt, :], ACT.Exp,
                                         scale=nA[:, dt, n:n + 1]).then_inc(dA_ready, 1)

            def scales(s):
                b, n = divmod(s, N)
                if n == 0:
                    wait_taken(act, "bc", b, 0)
                    for tt in range(TT):
                        wait_taken(act, "dxt", b, tt)
                if s >= 2:
                    act.wait_ge(dbx_ready, 4 * (s - 1))
                for tt in range(TT):
                    nc.scalar.activation(dxs[:, s % 2, tt], dx[b % 2][:, tt, :], ACT.Copy,
                                         scale=bct[:, b % 2, tt, R + n:R + n + 1]).then_inc(dxs_ready, 1)

            def front(n, b):
                ps = lambda *u: ps_misc[MISC[u][0]]
                if n == 10:
                    for i in range(DT):
                        take(("xnT", b, i), tr[:, i, :], ps("xnT", b, i))
                if n == 11:
                    take(("xdbl", b, 0), xdbl[:, :], ps("xdbl", b, 0)[0:XE, :])
                if n in (12, 13):
                    for i in (0, 1) if n == 12 else (2, 3):
                        wait_full(act, "draw", b, i)
                        nc.scalar.activation(soft[:, i], ps("draw", b, i), ACT.Abs, bias=bdt[:, i:i + 1]).then_inc(abs_ready, 1)
                if n == 13:
                    for i in range(DT):
                        act.wait_ge(abs_ready, 4 * b + i + 1)
                        nc.scalar.activation(soft[:, i], soft[:, i], ACT.Exp, scale=-1.0).then_inc(exp_ready, 1)
                if n == 14:
                    for i in range(DT):
                        act.wait_ge(exp_ready, 4 * b + i + 1)
                        if i >= 2:
                            act.wait_ge(log1p_ready, 4 * b + i - 1)
                        nc.scalar.activation(onep[:, i % 2], soft[:, i], ACT.Identity, bias=1.0).then_inc(onep_ready, 1)
                        if i % 2 == 1:
                            for j in (i - 1, i):
                                act.wait_ge(corr_ready, 4 * b + j + 1)
                                nc.scalar.activation(soft[:, j], soft[:, j], ACT.Ln, bias=1.0).then_inc(ln_ready, 1)
                if n == 15:
                    for i in range(TT):
                        take(("dxt", b, i), dx[b % 2][:, i, :], ps("dxt", b, i))

            def post(n, b):
                ps = lambda *u: ps_misc[MISC[u][0]]
                if n == 3:
                    act.wait_ge(dxT_ready, 4 * fronts(b))
                    for i in range(DT):
                        take(("x2T", b, i), tr[:, i, :], ps("x2T", b, i))
                if n == 4:
                    take(("lg", b, 0), lgT[:, :], ps("lg", b, 0)[0:E, :])
                if n == 5:
                    take(("sc", b, 0), score[:, :, :].rearrange("p a e -> p (a e)"), ps("sc", b, 0)[:, 0:TT * E],
                         ACT.Exp, scale=-1.0)
                i = {4: 0, 6: 1, 8: 2, 9: 3}.get(n)
                if i is not None:
                    wait_full(act, "g", b, i)
                    if i >= 2:
                        wait_taken(act, "u", b, i - 2)
                    nc.scalar.activation(onep[:, i % 2], ps("g", b, i), ACT.Tanh, scale=0.5).then_inc(tanh_ready, 1)
                for i in {10: (0,), 11: (1, 2), 12: (3,)}.get(n, ()):
                    k = b * TT + i
                    if k >= 2:
                        act.wait_ge(shared_stored[k % 2], 16 * (k // 2))
                    take(("dn", b, i), shout[:, k % 2], ps("dn", b, i))

            act.wait_ge(small_loaded, 16 * 7)
            nc.scalar.activation(nA[:, :, :], nA[:, :, :], ACT.Exp).then_inc(nA_exp, 1)
            for n in range(N):
                front(n, 0)
            exps(0)
            scales(0)
            for b in range(B):
                for n in range(N):
                    s = b * N + n
                    if n + 1 < N:
                        exps(s + 1)
                        scales(s + 1)
                    if b > 0:
                        post(n, b - 1)
                    if b + 1 < B:
                        front(n, b + 1)
                if b + 1 < B:
                    exps((b + 1) * N)
                    scales((b + 1) * N)
            for n in range(N):
                post(n, B - 1)

            def take_xgT(q, r):
                act.wait_ge(xg_turned, q * 4 + (r + 1))
                act.wait_ge(gu_ready, q * 4 + (r + 1))
                nc.scalar.activation(xgT[r % 2][:, :, 0:CAP], ps_xg[r % 2][:, 0:DT * CAP].rearrange("p (k c) -> p k c", k=DT),
                                     ACT.Copy).then_inc(xgT_ready, 1)

            def silu(q, r):
                act.wait_ge(gu_ready, q * 4 + (r + 3))
                act.wait_ge(hid_ready, q * 4 + (r + 1))
                nc.scalar.activation(sg[r % 2][:, :, :].rearrange("p a c -> p (a c)"), ps_gu[r % 2][:, 0:IT * CAPW], ACT.Silu).then_inc(silu_ready, 1)

            def weigh(q, r, first=False):
                e = q * 4 + r
                act.wait_ge(y_ready, q * 4 + (r + 3))
                if not first or r >= 2:
                    act.wait_ge(added, (q * 4 + (r - 1)) * 16)
                nc.scalar.activation(ye[r % 2][0:CAP, :], ps_y[r % 2][0:CAP, :], ACT.Copy,
                                     scale=slots[:, bass.ds(e, 1), 1:2].rearrange("c e k -> c (e k)").bitcast(F32)).then_inc(ye_ready, 1)

            act.sem_inc(xgT_ready, 2)
            act.sem_inc(ye_ready, 2)
            act.wait_ge(pad_ready, 2)
            act.wait_ge(slots_loaded, 16)
            take_xgT(0, 0)
            take_xgT(0, 1)
            silu(0, 0)
            for r in range(4):
                take_xgT(0, r + 2)
                silu(0, r + 1)
                weigh(0, r, first=True)
            with act.Fori(1, E // 4 - 1) as q:
                for r in range(4):
                    take_xgT(q, r + 2)
                    silu(q, r + 1)
                    weigh(q, r)
            for r in range(4):
                if r + 2 < 4:
                    take_xgT(E // 4 - 1, r + 2)
                if r + 1 < 4:
                    silu(E // 4 - 1, r + 1)
                weigh(E // 4 - 1, r)

        @block.vector
        def _(dve):
            steps = [0]

            def then(ins):
                steps[0] += 1
                ins.then_inc(dve_seq, 1)
                dve.wait_ge(dve_seq, steps[0])

            def variances(what, b, rows):
                place = PLACE[what]
                for tt in range(TT):
                    last = nc.vector.bn_stats(stat[:, place, tt, :], rows[:, tt, :])
                then(last)
                for tt in range(TT):
                    last = nc.vector.bn_aggr(mv[:, place, tt, :], stat[:, place, tt, :])
                last.then_inc(var_ready, 1)

            def normalise(what, b, rows, dst, done):
                place = PLACE[what]
                dve.wait_ge(rstd_ready, NORM[what, b] + 1)
                for tt in range(TT):
                    nc.vector.tensor_scalar(dst[:, tt, :], rows[:, tt, :], mv[:, place, tt, 0:1], rstd[:, place, tt:tt + 1],
                                            ALU.subtract, ALU.mult).then_inc(done, 1)

            def scan(s, dt):
                u = 4 * s + dt
                dve.wait_ge(dA_ready, u + 1)
                dve.wait_ge(dbx_ready, u + 1)
                if s >= 2:
                    dve.wait_ge(ht_ready, 4 * (s - 1))
                nc.vector.tensor_tensor_scan(h[:, s % 2, dt], dA[:, u % DA_RING], ps_dbx[dt][:, :], 0.0,
                                             ALU.mult, ALU.add).then_inc(h_ready, 1)

            def add_y(s, tt):
                b, n = divmod(s, N)
                u = 4 * s + tt
                dve.wait_ge(ht_ready, u + 1)
                if n == 0:
                    dve.wait_ge(y_init, 4 * b + tt + 1)
                else:
                    dve.wait_ge(y_added, u - 3)
                nc.vector.scalar_tensor_tensor(out=y[:, b % 2, tt], in0=ps_ht[u % 2][:, :],
                                               scalar=bct[:, b % 2, tt, R + N + n:R + N + n + 1], in1=y[:, b % 2, tt],
                                               op0=ALU.mult, op1=ALU.add).then_inc(y_added, 1)

            def front(n, b):
                if n == 4:
                    dve.wait_ge(x_loaded[b], 16)
                    variances("x", b, xall[:, b])
                if n == 6:
                    if b >= 2:
                        dve.wait_ge(x2_stored, 16 * (b - 1))
                        for i in range(DT):
                            wait_taken(dve, "x2T", b - 2, i)
                    normalise("x", b, xall[:, b], nrm, xn_ready)
                if n == 11:
                    ps = wait_full(dve, "bc", b, 0)
                    nc.vector.tensor_copy(bct[:, b % 2].rearrange("p a e -> p (a e)"), ps[:, 0:TT * XE]).then_inc(taken("bc", b, 0), 1)
                if n in (12, 13):
                    for i in (0, 1) if n == 12 else (2, 3):
                        dve.wait_ge(abs_ready, 4 * b + i + 1)
                        ps = ps_misc[MISC["draw", b, i][0]]
                        nc.vector.tensor_scalar(delta[b % 2][:, i, :], ps[:, :], bdt[:, i:i + 1], 0.0, ALU.add,
                                                ALU.max).then_inc(taken("draw", b, i), 1)
                if n == 14:
                    for i in range(DT):
                        dve.wait_ge(onep_ready, 4 * b + i + 1)
                        nc.vector.scalar_tensor_tensor(out=onep[:, i % 2], in0=onep[:, i % 2], scalar=1.0, in1=soft[:, i],
                                                       op0=ALU.subtract, op1=ALU.subtract).then_inc(corr_ready, 1)

            def hidden(b, i):
                dve.wait_ge(tanh_ready, 4 * b + i + 1)
                ps = wait_full(dve, "g", b, i)
                nc.vector.scalar_tensor_tensor(out=hs[:, i], in0=onep[:, i % 2], scalar=1.0, in1=ps[:, :],
                                               op0=ALU.add, op1=ALU.mult).then_inc(taken("g", b, i), 1)
                wait_taken(dve, "g", b, i)
                ps = wait_full(dve, "u", b, i)
                nc.vector.scalar_tensor_tensor(out=hs[:, i], in0=hs[:, i], scalar=0.5, in1=ps[:, :],
                                               op0=ALU.mult, op1=ALU.mult).then_inc(taken("u", b, i), 1)

            def best8(rows):
                for tt in range(TT):
                    last = nc.vector.max(top8[:, tt, :], rows(tt))
                then(last)
                for tt in range(TT):
                    last = nc.vector.max_index(top8i[:, tt, :], top8[:, tt, :], rows(tt))
                then(last)
                then(nc.vector.tensor_copy(topf[:, :, :], top8i[:, :, :]))

            def tile32(a):
                return a[:, :, :].rearrange("p a (g m) -> p (a g) m", m=EG)

            def choose(b):
                wait_taken(dve, "sc", b, 0)
                then(nc.vector.tensor_scalar(score[:, :, :], score[:, :, :], 1.0, None, ALU.add))
                then(nc.vector.reciprocal(score[:, :, :], score[:, :, :]))
                then(nc.vector.tensor_tensor(scb[:, :, :], score[:, :, :], ebias[:, :].unsqueeze(1).to_broadcast([P, TT, E]), ALU.add))
                v = tile32(scb)
                nc.vector.tensor_tensor(pair[:, 0], v[:, :, 0], v[:, :, 1], ALU.max)
                nc.vector.tensor_tensor(pair[:, 1], v[:, :, 2], v[:, :, 3], ALU.max)
                nc.vector.tensor_tensor(pair[:, 2], v[:, :, 0], v[:, :, 1], ALU.add)
                then(nc.vector.tensor_tensor(pair[:, 3], v[:, :, 2], v[:, :, 3], ALU.add))
                nc.vector.tensor_tensor(pair[:, 4], pair[:, 0], pair[:, 1], ALU.add)
                then(nc.vector.tensor_tensor(gs[:, :], pair[:, 2], pair[:, 3], ALU.max))
                then(nc.vector.tensor_tensor(gs[:, :], gs[:, :], pair[:, 4], ALU.max))
                best8(lambda tt: gs[:, tt * NG:(tt + 1) * NG])
                then(nc.vector.tensor_tensor(geq[:, :, :, :], topf[:, :, 0:TKG].unsqueeze(3).to_broadcast([P, TT, TKG, NG]),
                                             iota_e[:, 0:NG].unsqueeze(1).unsqueeze(1).to_broadcast([P, TT, TKG, NG]), ALU.is_equal))
                then(nc.vector.tensor_reduce(gmask[:, :, :], geq[:, :, :, :].rearrange("p a k g -> p a g k"), AX_X, ALU.add))
                then(nc.vector.tensor_tensor(v, v, gmask[:, :, :].rearrange("p a g -> p (a g)").unsqueeze(2).to_broadcast([P, TT * NG, EG]), ALU.mult))
                then(nc.vector.tensor_scalar(scb[:, :, :], scb[:, :, :], 0.0, None, ALU.add))
                best8(lambda tt: scb[:, tt, :])
                then(nc.vector.tensor_tensor(onehot[:, :, :, :], topf[:, :, 0:K].unsqueeze(3).to_broadcast([P, TT, K, E]),
                                             iota_e[:, :].unsqueeze(1).unsqueeze(1).to_broadcast([P, TT, K, E]), ALU.is_equal))
                nc.vector.tensor_reduce(mask[:, :, :], onehot[:, :, :, :].rearrange("p a k e -> p a e k"), AX_X, ALU.add).then_inc(mask_ready, 1)
                then(nc.vector.tensor_tensor(picked[:, :, :, :], onehot[:, :, :, :], score[:, :, :].unsqueeze(2).to_broadcast([P, TT, K, E]), ALU.mult))
                then(nc.vector.tensor_reduce(wsel[:, :, :], picked[:, :, :, :], AX_X, ALU.add))
                then(nc.vector.tensor_reduce(wsum[:, :], wsel[:, :, :], AX_X, ALU.add))
                then(nc.vector.tensor_scalar(wsum[:, :], wsum[:, :], 1e-20, None, ALU.add))
                then(nc.vector.reciprocal(wsum[:, :], wsum[:, :]))
                then(nc.vector.tensor_tensor(wsel[:, :, :], wsel[:, :, :], wsum[:, :].unsqueeze(2).to_broadcast([P, TT, K]), ALU.mult))

            def queue(b):
                ps = wait_full(dve, "mT", b, 0)
                nc.vector.tensor_tensor_scan(count[:, :], ones[:, :], ps[0:E, :], carry[:, 0:1], ALU.mult, ALU.add).then_inc(taken("mT", b, 0), 1)
                wait_taken(dve, "mT", b, 0)
                then(nc.vector.tensor_copy(carry[:, :], count[:, L - 1:L]))

            def destine(b):
                k = b % 2
                ps = wait_full(dve, "pos", b, 0)
                nc.vector.tensor_tensor(picked[:, :, :, :], onehot[:, :, :, :],
                                        ps[:, 0:TT * E].rearrange("p (a e) -> p a e", a=TT).unsqueeze(2).to_broadcast([P, TT, K, E]),
                                        ALU.mult).then_inc(taken("pos", b, 0), 1)
                wait_taken(dve, "pos", b, 0)
                then(nc.vector.tensor_reduce(possel[:, :, :], picked[:, :, :, :], AX_X, ALU.add))
                then(nc.vector.tensor_scalar(over[:, :, :], possel[:, :, :], float(CAP), BIG, ALU.is_gt, ALU.mult))
                then(nc.vector.tensor_tensor(over[:, :, :], over[:, :, :], possel[:, :, :], ALU.add))
                then(nc.vector.scalar_tensor_tensor(out=dest[:, :, :], in0=topf[:, :, 0:K], scalar=float(CAP), in1=over[:, :, :],
                                                    op0=ALU.mult, op1=ALU.add))
                if b >= 2:
                    dve.wait_ge(slots_written[k], 16 * TT * K * (b // 2))
                nc.vector.tensor_scalar(desti[:, k, :], dest[:, :, :].rearrange("p a k -> p (a k)"), -1.0, None, ALU.add)
                nc.vector.tensor_scalar(entry[:, k, :, :, 1].bitcast(F32), wsel[:, :, :], SCALE, None, ALU.mult)
                nc.vector.tensor_copy(entry[:, k, :, :, 0], tok[:, b * TT:(b + 1) * TT].unsqueeze(2).to_broadcast([P, TT, K])).then_inc(dest_ready, 1)

            def post(n, b):
                if n == 0:
                    dve.wait_ge(y_added, 4 * N * (b + 1))
                    variances("y", b, y[:, b % 2])
                if n == 1:
                    normalise("y", b, y[:, b % 2], y[:, b % 2], yn_ready)
                if n == 2:
                    dve.wait_ge(x1_ready, 4 * (b + 1))
                    variances("x1", b, xall[:, b])
                if n == 3:
                    dve.wait_ge(y_init, 4 * fronts(b))
                    for i in range(DT):
                        wait_taken(dve, "xnT", fronts(b) - 1, i)
                    normalise("x1", b, xall[:, b], nrm, x2_ready)
                if n == 6:
                    choose(b)
                if n == 8:
                    queue(b)
                if n == 9:
                    destine(b)
                i = {5: 0, 7: 1, 8: 2, 9: 3}.get(n)
                if i is not None:
                    hidden(b, i)

            nc.vector.memset(carry[:, :], 0.0)
            nc.vector.memset(ones[:, :], 1.0).then_inc(dve_const, 1)
            nc.vector.memset(y[0:CAP, 1, 0, :], 0.0).then_inc(dve_const, 1)
            front(4, 0)
            dve.wait_ge(nA_exp, 1)
            nc.vector.tensor_scalar(nA[:, :, :], nA[:, :, :], -1.0, None, ALU.mult).then_inc(nA_ready, 1)
            dve.wait_ge(pool_const, 7)
            for n in range(5, N):
                front(n, 0)
            for b in range(B):
                for n in range(N):
                    s = b * N + n
                    for j in range(4):
                        scan(s, j)
                        if s >= 1:
                            add_y(s - 1, j)
                    if b > 0:
                        post(n, b - 1)
                    if b + 1 < B:
                        front(n, b + 1)
            for j in range(4):
                add_y(B * N - 1, j)
            dve.wait_ge(y_added, 4 * N * B)
            for k in range(2):
                nc.vector.memset(xgT[k][:, :, CAP:CAPW], 0.0).then_inc(pad_ready, 1)
            for n in range(N):
                post(n, B - 1)

            def hide(q, r):
                dve.wait_ge(silu_ready, q * 4 + (r + 1))
                dve.wait_ge(y_ready, q * 4 + (r + 1))
                nc.vector.tensor_tensor(hid[r % 2][:, :, :].rearrange("p a c -> p (a c)"), sg[r % 2][:, :, :].rearrange("p a c -> p (a c)"),
                                        ps_gu[r % 2][:, IT * CAPW:2 * IT * CAPW], ALU.mult).then_inc(hid_ready, 1)

            dve.sem_inc(hid_ready, 2)
            with dve.Fori(0, E // 4) as q:
                for r in range(4):
                    hide(q, r)

            dve.wait_ge(fin_loaded[0], 16)
            variances("sum", 0, fin[0])
            for b in range(B):
                if b + 1 < B:
                    dve.wait_ge(fin_loaded[b + 1], 16)
                    dve.wait_ge(rstd_ready, NORM["sum", b] + 1)
                    normalise("sum", b, fin[b], fin[b], fin_normed)
                    dve.wait_ge(fin_normed, 4 * (b + 1))
                    variances("sum", b + 1, fin[b + 1])
                else:
                    normalise("sum", b, fin[b], fin[b], fin_normed)

        @block.gpsimd
        def _(pool):
            steps = [0]

            def then(ins):
                steps[0] += 1
                ins.then_inc(pool_seq, 1)
                pool.wait_ge(pool_seq, steps[0])

            def root(what, b):
                place = PLACE[what]
                pool.wait_ge(var_ready, NORM[what, b] + 1)
                then(nc.gpsimd.tensor_scalar(vpe[:, place, :], mv[:, place, :, 1], EPS, None, ALU.add))
                nc.gpsimd.tensor_tensor(rstd[:, place, :], vpe[:, place, :], mhalf[:, :], ALU.pow).then_inc(rstd_ready, 1)

            def front(n, b):
                if n == 5:
                    root("x", b)
                if n == 7:
                    if b == 1:
                        pool.wait_ge(filled, 48)
                    if b >= 2:
                        pool.wait_ge(x1_ready, 4 * (b - 1))
                    for tt in range(TT):
                        pool.wait_ge(xn_ready, 4 * b + tt + 1)
                        nc.gpsimd.tensor_tensor(y[:, b % 2, tt], nrm[:, tt, :], dbc[:, :], ALU.mult).then_inc(y_init, 1)
                if n == 14:
                    for i in range(DT):
                        pool.wait_ge(ln_ready, 4 * b + i + 1)
                        nc.gpsimd.tensor_tensor(soft[:, i], soft[:, i], onep[:, i % 2], ALU.subtract).then_inc(log1p_ready, 1)
                        pool.wait_ge(log1p_ready, 4 * b + i + 1)
                        wait_taken(pool, "draw", b, i)
                        nc.gpsimd.tensor_tensor(delta[b % 2][:, i, :], delta[b % 2][:, i, :], soft[:, i], ALU.add).then_inc(delta_ready, 1)
                        pool.wait_ge(delta_ready, 4 * b + i + 1)
                        nc.gpsimd.tensor_tensor(soft[:, i], delta[b % 2][:, i, :], tr[:, i, :], ALU.mult).then_inc(dxT_ready, 1)

            def post(n, b):
                if n == 0:
                    root("y", b)
                if n == 1:
                    for tt in range(TT):
                        pool.wait_ge(yn_ready, 4 * b + tt + 1)
                        nc.gpsimd.tensor_tensor(xall[:, b, tt], xall[:, b, tt], y[:, b % 2, tt], ALU.add).then_inc(x1_ready, 1)
                if n == 2:
                    root("x1", b)
                if n == 11:
                    k = b % 2
                    pool.wait_ge(dest_ready, b + 1)
                    if b == 0:
                        pool.wait_ge(filled, 48)
                    for j in range(TT * K):
                        nc.gpsimd.indirect_dma_start(
                            out=slot_table, out_offset=bass.IndirectOffsetOnAxis(ap=desti[:, k, j:j + 1].bitcast(U32), axis=0),
                            in_=entry[:, k, j // K, j % K, :], in_offset=None, bounds_check=SLOTS - 1,
                            oob_is_err=False).then_inc(slots_written[k], 16)

            nc.gpsimd.memset(ident[:, :], 0.0).then_inc(pool_const, 1)
            pool.wait_ge(pool_const, 1)
            nc.gpsimd.affine_select(out=ident[:, :], in_=ident[:, :], compare_op=ALU.not_equal, fill=1.0, base=0,
                                    pattern=[[-1, P]], channel_multiplier=1).then_inc(pool_const, 1)
            nc.gpsimd.memset(slots[:, :, :], 0).then_inc(pool_const, 1)
            pool.wait_ge(pool_const, 3)
            nc.gpsimd.iota(slots[:, :, 0], [[0, E]], base=T, channel_multiplier=1).then_inc(pool_const, 1)
            nc.gpsimd.iota(tok[:, :], [[P, B * TT]], base=0, channel_multiplier=1).then_inc(pool_const, 1)
            nc.gpsimd.iota(iota_e[:, :], [[1, E]], base=0, channel_multiplier=0, allow_small_or_imprecise_dtypes=True).then_inc(pool_const, 1)
            nc.gpsimd.memset(mhalf[:, :], -0.5).then_inc(pool_const, 1)
            pool.wait_ge(pool_const, 7)
            pool.wait_ge(small_loaded, 16 * 7)
            for n in range(N):
                front(n, 0)
            for b in range(B):
                for n in range(N):
                    if b > 0:
                        post(n, b - 1)
                    if b + 1 < B:
                        front(n, b + 1)
            for n in range(N):
                post(n, B - 1)

            def gather(e):
                if e >= 4:
                    pool.wait_ge(xg_turned, e - 3)
                nc.gpsimd.indirect_dma_start(
                    out=xg[e % 4][0:CAP, :], out_offset=None, in_=x2_rows,
                    in_offset=bass.IndirectOffsetOnAxis(ap=slots[:, e, 0:1].bitcast(U32), axis=0),
                    bounds_check=T + CAP - 1, oob_is_err=False).then_inc(gathered[e % 4], 16)

            def scatter_add(e):
                pool.wait_ge(ye_ready, e + 3)
                if e >= 1:
                    pool.wait_ge(added, e * 16)
                nc.gpsimd.indirect_dma_start(
                    out=ffn_rows, in_=ye[e % 2][0:CAP, :], in_offset=None,
                    out_offset=bass.IndirectOffsetOnAxis(ap=slots[:, e, 0:1].bitcast(U32), axis=0),
                    bounds_check=T + CAP - 1, oob_is_err=True, compute_op=ALU.add).then_inc(added, 16)

            pool.wait_ge(slots_loaded, 16)
            pool.wait_ge(x2_stored, 16 * B)
            for e in range(4):
                gather(e)
            for k in range(2):
                pool.wait_ge(shared_stored[k], 16 * TT * B // 2)
            for e in range(E):
                if e + 4 < E:
                    gather(e + 4)
                scatter_add(e)

            for b in range(B):
                root("sum", b)
                for tt in range(TT):
                    pool.wait_ge(fin_normed, 4 * b + tt + 1)
                    nc.gpsimd.tensor_tensor(fin[b][:, tt, :], fin[b][:, tt, :], xall[:, b, tt], ALU.add).then_inc(fin_ready, 1)


def kernel(L0_attn_x, L0_attn_W_xproj, L0_attn_W_dt, L0_attn_b_dt, L0_attn_A_log, L0_attn_D_param, L0_ffn_router_w,
           L0_ffn_e_bias, L0_ffn_W_gate, L0_ffn_W_up, L0_ffn_W_down, L0_ffn_shared_gate, L0_ffn_shared_up, L0_ffn_shared_down):
    import numpy as np
    import concourse.bacc as bacc
    from concourse import mybir as mb
    from concourse.bass_utils import run_bass_kernel_spmd

    def by_partition(w):
        w = np.asarray(w)
        e, rows, cols = w.shape
        return w.reshape(e, rows // 128, 128, cols).transpose(0, 2, 1, 3).reshape(e, 128, -1)

    arrays = {
        "x": np.asarray(L0_attn_x),
        "wxT": np.asarray(L0_attn_W_xproj).T,
        "wdT": np.asarray(L0_attn_W_dt).T,
        "b_dt": np.asarray(L0_attn_b_dt).reshape(DT, P).T,
        "A_log": np.asarray(L0_attn_A_log),
        "Dp": np.asarray(L0_attn_D_param),
        "rwT": np.asarray(L0_ffn_router_w).T,
        "e_bias": np.asarray(L0_ffn_e_bias),
        "wexp": np.concatenate([by_partition(L0_ffn_W_gate), by_partition(L0_ffn_W_up), by_partition(L0_ffn_W_down)], axis=2),
        "sgT": np.asarray(L0_ffn_shared_gate).T,
        "suT": np.asarray(L0_ffn_shared_up).T,
        "sdT": np.asarray(L0_ffn_shared_down).T,
    }
    nc = bacc.Bacc("TRN2", target_bir_lowering=False, num_devices=1)
    in_map, args = {}, {}
    for name, a in arrays.items():
        a = np.ascontiguousarray(a)
        in_map[f"in_{name}"] = a
        args[name] = nc.dram_tensor(f"in_{name}", a.shape, mb.dt.from_np(a.dtype), kind="ExternalInput").ap()
    args["out"] = nc.dram_tensor("out_0", (B, L, D), F32, kind="ExternalOutput").ap()
    sandwich(nc, **args)
    r = run_bass_kernel_spmd(nc, [in_map], core_ids=[0])
    return r.results[0]["out_0"]
```

```python
from contextlib import ExitStack

import concourse.bass as bass
from concourse import mybir

F32 = mybir.dt.float32
I32 = mybir.dt.int32
U32 = mybir.dt.uint32
ACT = mybir.ActivationFunctionType
ALU = mybir.AluOpType
AX_X = mybir.AxisListType.X

P = 128
B, L, D = 4, 512, 512
T = B * L
TT = L // P
DT = D // P
N = 16
R = 64
XE = R + 2 * N
E, K = 32, 4
NG, TKG = 8, 3
EG = E // NG
I = 256
IT = I // P
IS = 512
ST = IS // P
CAP = -(-T * 5 // (4 * E))
CAPW = 96
SLOTS = E * CAP
SCALE = 2.5
EPS = 1e-5
WE = DT * I * 2 + IT * D
WBUF = 4
DA_RING = 3
BC_RING = 4
POST_END = 20
BIG = 1.0e6


POST_WIDE = {6: ("lg", 0), **{8 + 2 * i: ("g", i) for i in range(ST)}, **{9 + 2 * i: ("u", i) for i in range(ST)},
             **{16 + i: ("dn", i) for i in range(TT)}}
FRONT_WIDE = {3: ("xdbl", 0)}
FRONT_DRAW = 5
POST_LIGHT = {**{(5, j): ("x2T", j) for j in range(4)}, (7, 0): ("sc", 0), (9, 1): ("mT", 0), (10, 0): ("pos", 0)}
FRONT_LIGHT = {**{(2, j): ("xnT", j) for j in range(4)}, **{(4, j): ("yi", j) for j in range(4)}, (6, 0): ("bc", 0)}


def beside(n, b):
    return ([("post", n + N, b - 2)] if b >= 2 and n + N < POST_END else []) + \
           ([("post", n, b - 1)] if b >= 1 else []) + ([("front", n, b + 1)] if b + 1 < B else [])


def slots_of_all():
    for n in range(N):
        for j in range(4):
            yield -1, n, j, [("front", n, 0)]
    for b in range(B):
        for n in range(N):
            for j in range(4):
                yield b, n, j, beside(n, b)
    for n in range(POST_END):
        for j in range(4):
            yield B, n, j, ([("post", n + N, B - 2)] if n + N < POST_END else []) + [("post", n, B - 1)]


def bank_turns():
    wide, light = [], []
    for _, _, j, pieces in slots_of_all():
        for piece, n, b in pieces:
            w = (POST_WIDE if piece == "post" else FRONT_WIDE).get(n)
            if w and j == 0:
                wide.append((w[0], b, w[1]))
            if piece == "front" and n == FRONT_DRAW:
                wide.append(("draw", b, j))
            li = (POST_LIGHT if piece == "post" else FRONT_LIGHT).get((n, j))
            if li:
                light.append((li[0], b, li[1]))
    return {**{u: (i % 2, i // 2) for i, u in enumerate(wide)}, **{u: (2, i) for i, u in enumerate(light)}}


MISC = bank_turns()


def norm_order():
    return [("x", b) for b in range(B)] + [(what, b) for b in range(B) for what in ("y", "x1")] + \
        [("sum", b) for b in range(B)]


NORM = {u: i for i, u in enumerate(norm_order())}


def norm_place(what, b):
    return {"x": b, "sum": b, "y": B, "x1": B + 1}[what]


def sandwich(nc, x, wxT, wdT, b_dt, A_log, Dp, rwT, e_bias, wexp, sgT, suT, sdT, out):
    with ExitStack() as ctx:
        def sb(name, shape, dt=F32):
            return ctx.enter_context(nc.sbuf_tensor(name, shape, dt))

        def sem(name):
            return ctx.enter_context(nc.semaphore(name))

        x2_rows = nc.dram_tensor("x2_rows", [T + CAP, D], F32).ap()
        ffn_rows = nc.dram_tensor("ffn_rows", [T + CAP, D], F32).ap()
        slot_table = nc.dram_tensor("slot_table", [SLOTS, 2], I32).ap()

        b_rows = nc.dram_tensor("b_rows", [B, N, L], F32).ap()

        arena = sb("arena", [P, WBUF * WE + 4 * D + 2 * (DT + 2 * IT) * CAPW + 2 * D])
        used = [0]

        def cut(n):
            used[0] += n
            assert used[0] <= arena.shape[1]
            return arena[:, used[0] - n:used[0]]
        delta = [cut(DT * L).rearrange("p (a l) -> p a l", a=DT) for _ in range(2)]
        xnT1 = cut(DT * L).rearrange("p (a l) -> p a l", a=DT)
        dbx = cut(2 * DT * L).rearrange("p (s a l) -> p s a l", s=2, a=DT)
        h = cut(2 * DT * L).rearrange("p (s a l) -> p s a l", s=2, a=DT)
        bcb = cut(BC_RING * L).rearrange("p (s l) -> p s l", s=BC_RING)
        wring = [arena[:, k * WE:(k + 1) * WE] for k in range(WBUF)]
        used[0] = WBUF * WE
        xg = [cut(D) for _ in range(4)]
        xgT = [cut(DT * CAPW).rearrange("p (a c) -> p a c", a=DT) for _ in range(2)]
        sg = [cut(IT * CAPW).rearrange("p (a c) -> p a c", a=IT) for _ in range(2)]
        hid = [cut(IT * CAPW).rearrange("p (a c) -> p a c", a=IT) for _ in range(2)]
        ye = [cut(D) for _ in range(2)]
        fin = [arena[:, k * TT * D:(k + 1) * TT * D].rearrange("p (a l) -> p a l", a=TT) for k in range(B)]

        xall = sb("xall", [P, B, TT, D])
        y = sb("y", [P, 2, TT, D])
        nrm = sb("nrm", [P, TT, D])
        onep = nrm
        xnT = [sb("xnT0", [P, DT, L]), xnT1]
        dxd = xnT
        tr = sb("tr", [P, DT, L])
        xdbl = sb("xdbl", [XE, L])
        bct = sb("bct", [P, 2, TT, XE])
        hs = sb("hs", [P, ST, L])
        soft = hs
        th = sb("th", [P, 2, L])
        shout = sb("shout", [P, 2, D])
        wx, wd, rw = sb("wx", [P, DT, XE]), sb("wd", [R, D]), sb("rw", [P, DT, E])
        wsg, wsu, wsd = sb("wsg", [P, DT, IS]), sb("wsu", [P, DT, IS]), sb("wsd", [P, ST, D])
        ebias, dcol = sb("ebias", [P, E]), sb("dcol", [P, DT])
        bdt, nA = sb("bdt", [P, DT]), sb("nA", [P, DT, N])
        ident, mhalf = sb("ident", [P, P]), sb("mhalf", [P, TT])
        iota_e, tok, ones = sb("iota_e", [P, E]), sb("tok", [P, B * TT], I32), sb("ones", [E, L])
        stat, mv = sb("stat", [P, B + 2, TT, 6]), sb("mv", [P, B + 2, TT, 2])
        vpe, rstd = sb("vpe", [P, B + 2, TT]), sb("rstd", [P, B + 2, TT])
        shift = sb("shift", [P, B + 2, TT])
        lgT, score, scb = sb("lgT", [E, L]), sb("score", [P, TT, E]), sb("scb", [P, TT, E])
        pair, gs = sb("pair", [P, 5, TT * NG]), sb("gs", [P, TT * NG])
        top8, top8i, topf = sb("top8", [P, TT, 8]), sb("top8i", [P, TT, 8], U32), sb("topf", [P, TT, 8])
        geq, gmask = sb("geq", [P, TT, TKG, NG]), sb("gmask", [P, TT, NG])
        onehot, picked = sb("onehot", [P, TT, K, E]), sb("picked", [P, TT, K, E])
        mask, count, carry = sb("mask", [P, TT, E]), sb("count", [E, L]), sb("carry", [E, 1])
        wsel, wsum = sb("wsel", [P, TT, K]), sb("wsum", [P, TT])
        possel, over, dest = sb("possel", [P, TT, K]), sb("over", [P, TT, K]), sb("dest", [P, TT, K])
        desti = sb("desti", [P, 2, TT * K], I32)
        entry = sb("entry", [P, 2, TT, K, 2], I32)
        slots = sb("slots", [CAP, E, 2], I32)

        def bank(name):
            return ctx.enter_context(nc.psum_tensor(name, [P, 512], F32))[:, :]
        ps_dA = [bank(f"ps_dA{i}") for i in range(DA_RING)]
        ps_ht = [bank(f"ps_ht{i}") for i in range(2)]
        ps_misc = [bank(f"ps_misc{i}") for i in range(3)]
        ps_xg, ps_gu, ps_y = ps_dA[0:2], [ps_dA[2], ps_misc[2]], ps_ht

        x_loaded = [sem(f"x_loaded{b}") for b in range(B)]
        small_loaded, shared_loaded = sem("small_loaded"), sem("shared_loaded")
        pool_const, dve_const = sem("pool_const"), sem("dve_const")
        nA_exp, nA_ready = sem("nA_exp"), sem("nA_ready")
        dA_ready, dbx_ready = sem("dA_ready"), sem("dbx_ready")
        b_stored, b_spread = sem("b_stored"), [sem(f"b_spread{k}") for k in range(BC_RING)]
        h_ready, ht_ready, y_added = sem("h_ready"), sem("ht_ready"), sem("y_added")
        misc_full = [sem(f"misc_full{k}") for k in range(3)]
        misc_taken = [sem(f"misc_taken{k}") for k in range(3)]
        dve_seq, pool_seq = sem("dve_seq"), sem("pool_seq")
        var_ready, rstd_ready = sem("var_ready"), sem("rstd_ready")
        xn_ready, xD_ready, relu_ready = sem("xn_ready"), sem("xD_ready"), sem("relu_ready")
        abs_ready, exp_ready, onep_ready = sem("abs_ready"), sem("exp_ready"), sem("onep_ready")
        corr_ready, ln_ready = sem("corr_ready"), sem("ln_ready")
        log1p_ready, delta_ready, dxd_ready = sem("log1p_ready"), sem("delta_ready"), sem("dxd_ready")
        yn_ready, x1_ready, x2_ready = sem("yn_ready"), sem("x1_ready"), sem("x2_ready")
        x2_stored = sem("x2_stored")
        mask_ready, dest_ready = sem("mask_ready"), sem("dest_ready")
        tanh_ready = sem("tanh_ready")
        shared_stored = [sem("shared_stored0"), sem("shared_stored1")]
        filled = sem("filled")
        slots_written = [sem("slots_written0"), sem("slots_written1")]
        slots_loaded = sem("slots_loaded")
        w_loaded = [sem(f"w_loaded{k}") for k in range(WBUF)]
        gathered = [sem(f"gathered{k}") for k in range(4)]
        xg_turned, silu_ready, pad_ready = sem("xg_turned"), sem("silu_ready"), sem("pad_ready")
        xgT_ready, gu_ready, hid_ready = sem("xgT_ready"), sem("gu_ready"), sem("hid_ready")
        y_ready, ye_ready, added = sem("y_ready"), sem("ye_ready"), sem("added")
        fin_loaded = [sem(f"fin_loaded{b}") for b in range(B)]
        fin_normed, fin_stored = sem("fin_normed"), sem("fin_stored")
        fin_ready = [sem(f"fin_ready{b}") for b in range(B)]

        def wait_full(eng, *u):
            k, turn = MISC[u]
            eng.wait_ge(misc_full[k], turn + 1)
            return ps_misc[k]

        def wait_taken(eng, *u):
            k, turn = MISC[u]
            eng.wait_ge(misc_taken[k], turn + 1)

        def taken(*u):
            return misc_taken[MISC[u][0]]

        def unit(b, n, j):
            return (b * N + n) * 4 + j

        block = ctx.enter_context(nc.Block())

        @block.sync
        def _(sp):
            xv = x.rearrange("b (t p) d -> b p t d", p=P)
            sp.dma_start(xall[:, 0], xv[0]).then_inc(x_loaded[0], 16)
            sp.dma_start(wx[:], wxT.rearrange("(t p) e -> p t e", p=P)).then_inc(small_loaded, 16)
            sp.dma_start(wd[:], wdT).then_inc(small_loaded, 16)
            sp.dma_start(bdt[:], b_dt).then_inc(small_loaded, 16)
            sp.dma_start(nA[:], A_log.rearrange("(t p) n -> p t n", p=P)).then_inc(small_loaded, 16)
            sp.dma_start(dcol[:], Dp).then_inc(small_loaded, 16)
            sp.dma_start(rw[:], rwT.rearrange("(t p) e -> p t e", p=P)).then_inc(small_loaded, 16)
            sp.dma_start(ebias[:], e_bias.partition_broadcast(P)).then_inc(small_loaded, 16)
            for b in range(1, B):
                sp.dma_start(xall[:, b], xv[b]).then_inc(x_loaded[b], 16)
            sp.dma_start(wsg[:], sgT.rearrange("(t p) i -> p t i", p=P)).then_inc(shared_loaded, 16)
            sp.dma_start(wsu[:], suT.rearrange("(t p) i -> p t i", p=P)).then_inc(shared_loaded, 16)
            sp.dma_start(wsd[:], sdT.rearrange("(t p) d -> p t d", p=P)).then_inc(shared_loaded, 16)
            sp.wait_ge(dve_const, 2)
            sp.wait_ge(pool_const, 4)
            sp.dma_start(x2_rows[T:T + CAP, :], y[0:CAP, 1, 0, :]).then_inc(filled, 16)
            sp.dma_start(ffn_rows[T:T + CAP, :], y[0:CAP, 1, 0, :]).then_inc(filled, 16)
            sp.dma_start(slot_table.rearrange("(e c) k -> c e k", c=CAP), slots[:]).then_inc(filled, 16)

            def spread(s):
                b, n = divmod(s, N)
                if n == 0:
                    sp.wait_ge(b_stored, 16 * (b + 1))
                if s >= BC_RING:
                    sp.wait_ge(dbx_ready, 4 * (s - BC_RING + 1))
                sp.dma_start(bcb[:, s % BC_RING], b_rows[b, n].partition_broadcast(P)).then_inc(b_spread[s % BC_RING], 16)

            def front(n, b):
                if n == 4:
                    wait_taken(sp, "xdbl", b, 0)
                    sp.dma_start(b_rows[b], xdbl[R:R + N, :]).then_inc(b_stored, 16)

            def post(n, b):
                if n == 5:
                    sp.wait_ge(x2_ready, 4 * (b + 1))
                    sp.dma_start(x2_rows[b * L:(b + 1) * L, :].rearrange("(t p) d -> p t d", p=P), nrm[:]).then_inc(x2_stored, 16)
                if n >= 16:
                    k = b * TT + n - 16
                    wait_taken(sp, "dn", b, n - 16)
                    sp.dma_start(ffn_rows[k * P:(k + 1) * P, :], shout[:, k % 2]).then_inc(shared_stored[k % 2], 16)

            for b, n, j, pieces in slots_of_all():
                if j != 3:
                    continue
                if b == B and 4 <= n < 4 + WBUF:
                    sp.wait_ge(y_added, 4 * N * B)
                    sp.dma_start(wring[n - 4], wexp[n - 4]).then_inc(w_loaded[n - 4], 16)
                if b == B and n == 16:
                    for k in range(2):
                        sp.wait_ge(slots_written[k], 16 * TT * K * B // 2)
                    sp.dma_start(slots[:], slot_table.rearrange("(e c) k -> c e k", c=CAP)).then_inc(slots_loaded, 16)
                for piece, m, c in pieces:
                    (front if piece == "front" else post)(m, c)
                s = b * N + n
                if 0 <= s + 3 < B * N:
                    spread(s + 3)
            with sp.Fori(1, E // WBUF) as q:
                for k in range(WBUF):
                    sp.wait_ge(y_ready, q * WBUF + (k - WBUF + 3))
                    sp.dma_start(wring[k], wexp[bass.ds(q * WBUF + k, 1)].rearrange("a p w -> (a p) w")).then_inc(w_loaded[k], 16)
            sp.wait_ge(added, 16 * E)
            for b in range(B):
                rows = ffn_rows[b * L:(b + 1) * L, :].rearrange("(t p) d -> p t d", p=P)
                sp.dma_start(fin[b], rows).then_inc(fin_loaded[b], 16)
            ov = out.rearrange("b (t p) d -> b p t d", p=P)
            for b in range(B):
                sp.wait_ge(fin_ready[b], TT)
                sp.dma_start(ov[b], fin[b]).then_inc(fin_stored, 16)
            sp.wait_ge(fin_stored, 16 * B)

        @block.tensor
        def _(pe):
            def turn4(dst, full, src, width=P):
                for j in range(4):
                    k = src(j).shape[0]
                    last = nc.tensor.transpose(dst[0:src(j).shape[1], j * width:j * width + k], src(j), ident[0:k, 0:k])
                last.then_inc(full, 1)

            def open_bank(u):
                k, turn = MISC[u]
                if turn > 0:
                    pe.wait_ge(misc_taken[k], turn)
                return ps_misc[k], misc_full[k]

            def wide(name, b, i, j):
                ps = open_bank((name, b, i))[0] if j == 0 else ps_misc[MISC[name, b, i][0]]
                full = misc_full[MISC[name, b, i][0]]
                dst = ps[:, :]
                if name == "xdbl":
                    wait_taken(pe, "xnT", b, j)
                    dst, w, v = ps[0:XE, :], wx[:, j, :], xnT[b % 2][:, j, :]
                elif name == "lg":
                    wait_taken(pe, "x2T", b, j)
                    dst, w, v = ps[0:E, :], rw[:, j, :], tr[:, j, :]
                elif name in ("g", "u"):
                    w, v = (wsg if name == "g" else wsu)[:, j, i * P:(i + 1) * P], tr[:, j, :]
                else:
                    wait_taken(pe, "u", b, j)
                    w, v = hs[:, j, i * P:(i + 1) * P], wsd[:, j, :]
                last = nc.tensor.matmul(dst, w, v, start=(j == 0), stop=(j == 3))
                if j == 3:
                    last.then_inc(full, 1)

            def light(name, b, i):
                ps, full = open_bank((name, b, i))
                if name == "xnT":
                    pe.wait_ge(xn_ready, 4 * (b + 1))
                    turn4(ps, full, lambda tt: nrm[:, tt, i * P:(i + 1) * P])
                elif name == "yi":
                    pe.wait_ge(xD_ready, 4 * (b + 1))
                    turn4(ps, full, lambda dt: tr[:, dt, i * P:(i + 1) * P])
                elif name == "bc":
                    wait_taken(pe, "xdbl", b, 0)
                    for tt in range(TT):
                        last = nc.tensor.transpose(ps[:, tt * XE:(tt + 1) * XE], xdbl[:, tt * P:(tt + 1) * P], ident[0:XE, 0:XE])
                    last.then_inc(full, 1)
                elif name == "draw":
                    wait_taken(pe, "xdbl", b, 0)
                    nc.tensor.matmul(ps[:, :], wd[:, i * P:(i + 1) * P], xdbl[0:R, :], start=True, stop=True).then_inc(full, 1)
                elif name == "x2T":
                    pe.wait_ge(x2_ready, 4 * (b + 1))
                    turn4(ps, full, lambda tt: nrm[:, tt, i * P:(i + 1) * P])
                elif name == "sc":
                    wait_taken(pe, "lg", b, 0)
                    for tt in range(TT):
                        last = nc.tensor.transpose(ps[:, tt * E:(tt + 1) * E], lgT[:, tt * P:(tt + 1) * P], ident[0:E, 0:E])
                    last.then_inc(full, 1)
                elif name == "mT":
                    pe.wait_ge(mask_ready, b + 1)
                    for tt in range(TT):
                        last = nc.tensor.transpose(ps[0:E, tt * P:(tt + 1) * P], mask[:, tt, :], ident[:, :])
                    last.then_inc(full, 1)
                else:
                    wait_taken(pe, "mT", b, 0)
                    for tt in range(TT):
                        last = nc.tensor.transpose(ps[:, tt * E:(tt + 1) * E], count[:, tt * P:(tt + 1) * P], ident[0:E, 0:E])
                    last.then_inc(full, 1)

            def turn_h(u):
                s, tt = divmod(u, 4)
                pe.wait_ge(h_ready, 4 * (s + 1))
                if u >= 2:
                    pe.wait_ge(y_added, u - 1)
                turn4(ps_ht[u % 2], ht_ready, lambda dt: h[:, s % 2, dt, tt * P:(tt + 1) * P])

            pe.wait_ge(pool_const, 2)
            pe.wait_ge(small_loaded, 16 * 7)
            for b, n, j, pieces in slots_of_all():
                u = unit(b, n, j) - 4
                if 0 <= u < 4 * N * B:
                    turn_h(u)
                for piece, m, c in pieces:
                    if m == 8 and piece == "post" and j == 0:
                        pe.wait_ge(shared_loaded, 16 * 3)
                    li = (POST_LIGHT if piece == "post" else FRONT_LIGHT).get((m, j))
                    if li:
                        light(li[0], c, li[1])
                    if piece == "front" and m == FRONT_DRAW:
                        light("draw", c, j)
                    w = (POST_WIDE if piece == "post" else FRONT_WIDE).get(m)
                    if w:
                        wide(w[0], c, w[1], j)

            def turn_xg(q, r):
                pe.wait_ge(gathered[r % 4], (q + r // 4 + 1) * 16)
                pe.wait_ge(xgT_ready, q * 4 + (r + 1))
                for k in range(DT):
                    last = nc.tensor.transpose(ps_xg[r % 2][:, k * CAP:(k + 1) * CAP],
                                               xg[r % 4][0:CAP, k * P:(k + 1) * P], ident[0:CAP, 0:CAP])
                last.then_inc(xg_turned, 1)

            def gate_up(q, r):
                w = wring[r % WBUF][:, 0:2 * DT * I].rearrange("p (m k i) -> p m k i", m=2, k=DT)
                pe.wait_ge(w_loaded[r % WBUF], (q + r // WBUF + 1) * 16)
                pe.wait_ge(xgT_ready, q * 4 + (r + 3))
                pe.wait_ge(hid_ready, q * 4 + (r + 1))
                for m in range(2):
                    for it in range(IT):
                        c = (m * IT + it) * CAPW
                        for k in range(DT):
                            last = nc.tensor.matmul(ps_gu[r % 2][:, c:c + CAPW], w[:, m, k, it * P:(it + 1) * P],
                                                    xgT[r % 2][:, k, :], start=(k == 0), stop=(k == DT - 1))
                last.then_inc(gu_ready, 1)

            def down(q, r):
                w = wring[r % WBUF][:, 2 * DT * I:].rearrange("p (k d) -> p k d", k=IT)
                pe.wait_ge(hid_ready, q * 4 + (r + 3))
                pe.wait_ge(ye_ready, q * 4 + (r + 1))
                for k in range(IT):
                    last = nc.tensor.matmul(ps_y[r % 2][0:CAP, :], hid[r % 2][:, k, 0:CAP], w[:, k, :],
                                            start=(k == 0), stop=(k == IT - 1))
                last.then_inc(y_ready, 1)

            pe.sem_inc(gu_ready, 2)
            pe.sem_inc(y_ready, 2)
            pe.wait_ge(pad_ready, 2)
            turn_xg(0, 0)
            turn_xg(0, 1)
            gate_up(0, 0)
            with pe.Fori(0, E // 4 - 1) as q:
                for r in range(4):
                    turn_xg(q, r + 2)
                    gate_up(q, r + 1)
                    down(q, r)
            for r in range(4):
                if r + 2 < 4:
                    turn_xg(E // 4 - 1, r + 2)
                if r + 1 < 4:
                    gate_up(E // 4 - 1, r + 1)
                down(E // 4 - 1, r)

        @block.scalar
        def _(act):
            def take(u, dst, src, func=ACT.Copy, **kw):
                wait_full(act, *u)
                nc.scalar.activation(dst, src, func, **kw).then_inc(taken(*u), 1)

            def ps(*u):
                return ps_misc[MISC[u][0]]

            def exp_dA(u):
                (b, n), dt = divmod(u // 4, N), u % 4
                if n == 0 and dt == 0:
                    act.wait_ge(delta_ready, 4 * (b + 1))
                if u >= DA_RING:
                    act.wait_ge(h_ready, u - DA_RING + 1)
                nc.scalar.activation(ps_dA[u % DA_RING], delta[b % 2][:, dt, :], ACT.Exp, scale=nA[:, dt, n:n + 1]).then_inc(dA_ready, 1)

            def normalise(what, b, tt, rows, dst, done):
                place = norm_place(what, b)
                if tt == 0:
                    act.wait_ge(rstd_ready, NORM[what, b] + 1)
                nc.scalar.activation(dst, rows, ACT.Identity, bias=shift[:, place, tt:tt + 1], scale=rstd[:, place, tt:tt + 1]).then_inc(done, 1)

            def front(n, j, b):
                if n == 1:
                    if b >= 1 and j == 0:
                        act.wait_ge(log1p_ready, 4 * b)
                    normalise("x", b, j, xall[:, b, j], nrm[:, j, :], xn_ready)
                if n == 2:
                    if b >= 2 and j == 0:
                        act.wait_ge(dbx_ready, 4 * N * (b - 1))
                    take(("xnT", b, j), xnT[b % 2][:, j, :], ps("xnT", b, j))
                if n == 3:
                    wait_taken(act, "xnT", b, j)
                    nc.scalar.activation(tr[:, j, :], xnT[b % 2][:, j, :], ACT.Copy, scale=dcol[:, j:j + 1]).then_inc(xD_ready, 1)
                    if j == 3:
                        take(("xdbl", b, 0), xdbl[:, :], ps("xdbl", b, 0)[0:XE, :])
                if n == 4:
                    if b >= 2 and j == 0:
                        act.wait_ge(x1_ready, 4 * (b - 1))
                    if b == 1 and j == 0:
                        act.wait_ge(filled, 48)
                    take(("yi", b, j), y[:, b % 2, j], ps("yi", b, j))
                if n == 5:
                    wait_full(act, "draw", b, j)
                    nc.scalar.activation(soft[:, j], ps("draw", b, j), ACT.Abs, bias=bdt[:, j:j + 1]).then_inc(abs_ready, 1)
                    nc.scalar.activation(delta[b % 2][:, j, :], ps("draw", b, j), ACT.Relu, bias=bdt[:, j:j + 1]).then_inc(taken("draw", b, j), 1)
                if n == 6:
                    act.wait_ge(abs_ready, 4 * b + j + 1)
                    nc.scalar.activation(soft[:, j], soft[:, j], ACT.Exp, scale=-1.0).then_inc(exp_ready, 1)
                if n == 7:
                    act.wait_ge(exp_ready, 4 * b + j + 1)
                    if b >= 2 and j == 0:
                        act.wait_ge(x2_stored, 16 * (b - 1))
                        wait_full(act, "x2T", b - 2, 3)
                    nc.scalar.activation(onep[:, j, :], soft[:, j], ACT.Identity, bias=1.0).then_inc(onep_ready, 1)
                if n == 8 and j == 0:
                    for i in range(DT):
                        act.wait_ge(corr_ready, 4 * b + i + 1)
                        nc.scalar.activation(soft[:, i], soft[:, i], ACT.Ln, bias=1.0).then_inc(ln_ready, 1)

            def post(n, j, b):
                if n == 2:
                    normalise("y", b, j, y[:, b % 2, j], y[:, b % 2, j], yn_ready)
                if n == 4:
                    normalise("x1", b, j, xall[:, b, j], nrm[:, j, :], x2_ready)
                if n == 5:
                    take(("x2T", b, j), tr[:, j, :], ps("x2T", b, j))
                if (n, j) == (6, 3):
                    take(("lg", b, 0), lgT[:, :], ps("lg", b, 0)[0:E, :])
                if (n, j) == (7, 0):
                    take(("sc", b, 0), score[:, :, :].rearrange("p a e -> p (a e)"), ps("sc", b, 0)[:, 0:TT * E],
                         ACT.Exp, scale=-1.0)
                if n in (9, 11, 13, 15) and j == 0:
                    i = (n - 9) // 2
                    wait_full(act, "g", b, i)
                    if 4 * b + i >= 2:
                        wait_taken(act, "g", *divmod(4 * b + i - 2, 4))
                    nc.scalar.activation(th[:, i % 2], ps("g", b, i), ACT.Tanh, scale=0.5).then_inc(tanh_ready, 1)
                if n >= 16 and j == 3:
                    i = n - 16
                    k = b * TT + i
                    if k >= 2:
                        act.wait_ge(shared_stored[k % 2], 16 * (k // 2))
                    take(("dn", b, i), shout[:, k % 2], ps("dn", b, i))

            act.wait_ge(small_loaded, 16 * 7)
            nc.scalar.activation(nA[:, :, :], nA[:, :, :], ACT.Exp).then_inc(nA_exp, 1)
            for b, n, j, pieces in slots_of_all():
                u = unit(b, n, j) + DA_RING - 1
                if u >= 0 and b < B and u < 4 * N * B:
                    if u == 0:
                        act.wait_ge(nA_ready, 1)
                    exp_dA(u)
                for piece, m, c in pieces:
                    (front if piece == "front" else post)(m, j, c)

            def take_xgT(q, r):
                act.wait_ge(xg_turned, q * 4 + (r + 1))
                act.wait_ge(gu_ready, q * 4 + (r + 1))
                nc.scalar.activation(xgT[r % 2][:, :, 0:CAP], ps_xg[r % 2][:, 0:DT * CAP].rearrange("p (k c) -> p k c", k=DT),
                                     ACT.Copy).then_inc(xgT_ready, 1)

            def silu(q, r):
                act.wait_ge(gu_ready, q * 4 + (r + 3))
                act.wait_ge(hid_ready, q * 4 + (r + 1))
                nc.scalar.activation(sg[r % 2][:, :, :].rearrange("p a c -> p (a c)"), ps_gu[r % 2][:, 0:IT * CAPW], ACT.Silu).then_inc(silu_ready, 1)

            def weigh(q, r, first=False):
                e = q * 4 + r
                act.wait_ge(y_ready, q * 4 + (r + 3))
                if not first or r >= 2:
                    act.wait_ge(added, (q * 4 + (r - 1)) * 16)
                nc.scalar.activation(ye[r % 2][0:CAP, :], ps_y[r % 2][0:CAP, :], ACT.Copy,
                                     scale=slots[:, bass.ds(e, 1), 1:2].rearrange("c e k -> c (e k)").bitcast(F32)).then_inc(ye_ready, 1)

            act.sem_inc(xgT_ready, 2)
            act.sem_inc(ye_ready, 2)
            act.wait_ge(pad_ready, 2)
            act.wait_ge(slots_loaded, 16)
            take_xgT(0, 0)
            take_xgT(0, 1)
            silu(0, 0)
            for r in range(4):
                take_xgT(0, r + 2)
                silu(0, r + 1)
                weigh(0, r, first=True)
            with act.Fori(1, E // 4 - 1) as q:
                for r in range(4):
                    take_xgT(q, r + 2)
                    silu(q, r + 1)
                    weigh(q, r)
            for r in range(4):
                if r + 2 < 4:
                    take_xgT(E // 4 - 1, r + 2)
                if r + 1 < 4:
                    silu(E // 4 - 1, r + 1)
                weigh(E // 4 - 1, r)

            for b in range(B):
                for tt in range(TT):
                    normalise("sum", b, tt, fin[b][:, tt, :], fin[b][:, tt, :], fin_normed)

        @block.vector
        def _(dve):
            steps = [0]

            def then(ins):
                steps[0] += 1
                ins.then_inc(dve_seq, 1)
                dve.wait_ge(dve_seq, steps[0])

            def variance(what, b, tt, rows):
                place = norm_place(what, b)
                last = nc.vector.bn_stats(stat[:, place, tt, :], rows)
                if tt == TT - 1:
                    then(last)
                    for t in range(TT):
                        last = nc.vector.bn_aggr(mv[:, place, t, :], stat[:, place, t, :])
                    last.then_inc(var_ready, 1)

            def scan(u):
                s, dt = divmod(u, 4)
                dve.wait_ge(dA_ready, u + 1)
                dve.wait_ge(dbx_ready, u + 1)
                if s >= 2:
                    dve.wait_ge(ht_ready, 4 * (s - 1))
                nc.vector.tensor_tensor_scan(h[:, s % 2, dt], ps_dA[u % DA_RING], dbx[:, s % 2, dt, :], 0.0,
                                             ALU.mult, ALU.add).then_inc(h_ready, 1)

            def add_y(u):
                (b, n), tt = divmod(u // 4, N), u % 4
                dve.wait_ge(ht_ready, u + 1)
                if n == 0:
                    wait_taken(dve, "yi", b, tt)
                else:
                    dve.wait_ge(y_added, u - 3)
                nc.vector.scalar_tensor_tensor(out=y[:, b % 2, tt], in0=ps_ht[u % 2][:, :],
                                               scalar=bct[:, b % 2, tt, R + N + n:R + N + n + 1], in1=y[:, b % 2, tt],
                                               op0=ALU.mult, op1=ALU.add).then_inc(y_added, 1)

            def add_delta(b, i):
                dve.wait_ge(log1p_ready, 4 * b + i + 1)
                nc.vector.tensor_tensor(delta[b % 2][:, i, :], delta[b % 2][:, i, :], soft[:, i], ALU.add).then_inc(delta_ready, 1)

            def front(n, j, b):
                if b == 0 and n < B:
                    if j == 0:
                        dve.wait_ge(x_loaded[n], 16)
                    variance("x", n, j, xall[:, n, j, :])
                if (n, j) == (6, 1):
                    ps = wait_full(dve, "bc", b, 0)
                    nc.vector.tensor_copy(bct[:, b % 2].rearrange("p a e -> p (a e)"), ps[:, 0:TT * XE]).then_inc(taken("bc", b, 0), 1)
                if n == 7:
                    dve.wait_ge(onep_ready, 4 * b + j + 1)
                    nc.vector.scalar_tensor_tensor(out=onep[:, j], in0=onep[:, j], scalar=1.0, in1=soft[:, j],
                                                   op0=ALU.subtract, op1=ALU.subtract).then_inc(corr_ready, 1)
                if n == 8 and b == 0:
                    dve.wait_ge(ln_ready, j + 1)
                    nc.vector.tensor_tensor(soft[:, j], soft[:, j], onep[:, j], ALU.subtract).then_inc(log1p_ready, 1)
                    add_delta(b, j)
                    dve.wait_ge(delta_ready, j + 1)
                    nc.vector.tensor_tensor(dxd[b % 2][:, j, :], delta[b % 2][:, j, :], xnT[b % 2][:, j, :], ALU.mult).then_inc(dxd_ready, 1)
                if n == 9 and b > 0:
                    add_delta(b, j)

            def hidden_gate(b, i):
                dve.wait_ge(tanh_ready, 4 * b + i + 1)
                ps = ps_misc[MISC["g", b, i][0]]
                if b + 2 < B:
                    dve.wait_ge(delta_ready, 4 * (b + 2) + i + 1)
                nc.vector.scalar_tensor_tensor(out=hs[:, i], in0=th[:, i % 2], scalar=1.0, in1=ps[:, :],
                                               op0=ALU.add, op1=ALU.mult).then_inc(taken("g", b, i), 1)

            def hidden_up(b, i):
                wait_taken(dve, "g", b, i)
                ps = wait_full(dve, "u", b, i)
                nc.vector.scalar_tensor_tensor(out=hs[:, i], in0=hs[:, i], scalar=0.5, in1=ps[:, :],
                                               op0=ALU.mult, op1=ALU.mult).then_inc(taken("u", b, i), 1)

            def best8(rows):
                for tt in range(TT):
                    last = nc.vector.max(top8[:, tt, :], rows(tt))
                then(last)
                for tt in range(TT):
                    last = nc.vector.max_index(top8i[:, tt, :], top8[:, tt, :], rows(tt))
                then(last)
                then(nc.vector.tensor_copy(topf[:, :, :], top8i[:, :, :]))

            def tile32(a):
                return a[:, :, :].rearrange("p a (g m) -> p (a g) m", m=EG)

            def choose(b):
                wait_taken(dve, "sc", b, 0)
                then(nc.vector.tensor_scalar(score[:, :, :], score[:, :, :], 1.0, None, ALU.add))
                then(nc.vector.reciprocal(score[:, :, :], score[:, :, :]))
                then(nc.vector.tensor_tensor(scb[:, :, :], score[:, :, :], ebias[:, :].unsqueeze(1).to_broadcast([P, TT, E]), ALU.add))
                v = tile32(scb)
                nc.vector.tensor_tensor(pair[:, 0], v[:, :, 0], v[:, :, 1], ALU.max)
                nc.vector.tensor_tensor(pair[:, 1], v[:, :, 2], v[:, :, 3], ALU.max)
                nc.vector.tensor_tensor(pair[:, 2], v[:, :, 0], v[:, :, 1], ALU.add)
                then(nc.vector.tensor_tensor(pair[:, 3], v[:, :, 2], v[:, :, 3], ALU.add))
                nc.vector.tensor_tensor(pair[:, 4], pair[:, 0], pair[:, 1], ALU.add)
                then(nc.vector.tensor_tensor(gs[:, :], pair[:, 2], pair[:, 3], ALU.max))
                then(nc.vector.tensor_tensor(gs[:, :], gs[:, :], pair[:, 4], ALU.max))
                best8(lambda tt: gs[:, tt * NG:(tt + 1) * NG])
                then(nc.vector.tensor_tensor(geq[:, :, :, :], topf[:, :, 0:TKG].unsqueeze(3).to_broadcast([P, TT, TKG, NG]),
                                             iota_e[:, 0:NG].unsqueeze(1).unsqueeze(1).to_broadcast([P, TT, TKG, NG]), ALU.is_equal))
                then(nc.vector.tensor_reduce(gmask[:, :, :], geq[:, :, :, :].rearrange("p a k g -> p a g k"), AX_X, ALU.add))
                then(nc.vector.tensor_tensor(v, v, gmask[:, :, :].rearrange("p a g -> p (a g)").unsqueeze(2).to_broadcast([P, TT * NG, EG]), ALU.mult))
                then(nc.vector.tensor_scalar(scb[:, :, :], scb[:, :, :], 0.0, None, ALU.add))
                best8(lambda tt: scb[:, tt, :])
                then(nc.vector.tensor_tensor(onehot[:, :, :, :], topf[:, :, 0:K].unsqueeze(3).to_broadcast([P, TT, K, E]),
                                             iota_e[:, :].unsqueeze(1).unsqueeze(1).to_broadcast([P, TT, K, E]), ALU.is_equal))
                nc.vector.tensor_reduce(mask[:, :, :], onehot[:, :, :, :].rearrange("p a k e -> p a e k"), AX_X, ALU.add).then_inc(mask_ready, 1)
                then(nc.vector.tensor_tensor(picked[:, :, :, :], onehot[:, :, :, :], score[:, :, :].unsqueeze(2).to_broadcast([P, TT, K, E]), ALU.mult))
                then(nc.vector.tensor_reduce(wsel[:, :, :], picked[:, :, :, :], AX_X, ALU.add))
                then(nc.vector.tensor_reduce(wsum[:, :], wsel[:, :, :], AX_X, ALU.add))
                then(nc.vector.tensor_scalar(wsum[:, :], wsum[:, :], 1e-20, None, ALU.add))
                then(nc.vector.reciprocal(wsum[:, :], wsum[:, :]))
                then(nc.vector.tensor_tensor(wsel[:, :, :], wsel[:, :, :], wsum[:, :].unsqueeze(2).to_broadcast([P, TT, K]), ALU.mult))

            def queue(b):
                ps = wait_full(dve, "mT", b, 0)
                nc.vector.tensor_tensor_scan(count[:, :], ones[:, :], ps[0:E, :], carry[:, 0:1], ALU.mult, ALU.add).then_inc(taken("mT", b, 0), 1)
                wait_taken(dve, "mT", b, 0)
                then(nc.vector.tensor_copy(carry[:, :], count[:, L - 1:L]))

            def destine(b):
                k = b % 2
                ps = wait_full(dve, "pos", b, 0)
                nc.vector.tensor_tensor(picked[:, :, :, :], onehot[:, :, :, :],
                                        ps[:, 0:TT * E].rearrange("p (a e) -> p a e", a=TT).unsqueeze(2).to_broadcast([P, TT, K, E]),
                                        ALU.mult).then_inc(taken("pos", b, 0), 1)
                wait_taken(dve, "pos", b, 0)
                then(nc.vector.tensor_reduce(possel[:, :, :], picked[:, :, :, :], AX_X, ALU.add))
                then(nc.vector.tensor_scalar(over[:, :, :], possel[:, :, :], float(CAP), BIG, ALU.is_gt, ALU.mult))
                then(nc.vector.tensor_tensor(over[:, :, :], over[:, :, :], possel[:, :, :], ALU.add))
                then(nc.vector.scalar_tensor_tensor(out=dest[:, :, :], in0=topf[:, :, 0:K], scalar=float(CAP), in1=over[:, :, :],
                                                    op0=ALU.mult, op1=ALU.add))
                if b >= 2:
                    dve.wait_ge(slots_written[k], 16 * TT * K * (b // 2))
                nc.vector.tensor_scalar(desti[:, k, :], dest[:, :, :].rearrange("p a k -> p (a k)"), -1.0, None, ALU.add)
                nc.vector.tensor_scalar(entry[:, k, :, :, 1].bitcast(F32), wsel[:, :, :], SCALE, None, ALU.mult)
                nc.vector.tensor_copy(entry[:, k, :, :, 0], tok[:, b * TT:(b + 1) * TT].unsqueeze(2).to_broadcast([P, TT, K])).then_inc(dest_ready, 1)

            def add_x(b, tt):
                dve.wait_ge(yn_ready, 4 * b + tt + 1)
                nc.vector.tensor_tensor(xall[:, b, tt], xall[:, b, tt], y[:, b % 2, tt], ALU.add).then_inc(x1_ready, 1)

            def post(n, j, b):
                if n == 1:
                    if j == 0:
                        dve.wait_ge(y_added, 4 * N * (b + 1))
                    variance("y", b, j, y[:, b % 2, j])
                if n == 2 and j > 0:
                    add_x(b, j - 1)
                if n == 3:
                    if j == 0:
                        add_x(b, 3)
                    dve.wait_ge(x1_ready, 4 * b + (4 if j else 3))
                    variance("x1", b, j, xall[:, b, j])
                if (n, j) == (8, 0):
                    choose(b)
                if (n, j) == (9, 2):
                    queue(b)
                if (n, j) == (10, 1):
                    destine(b)
                if n in (9, 11, 13, 15) and j == 1:
                    hidden_gate(b, (n - 9) // 2)
                if n in (10, 12, 14, 16) and j == 0:
                    hidden_up(b, (n - 10) // 2)

            nc.vector.memset(carry[:, :], 0.0)
            nc.vector.memset(ones[:, :], 1.0).then_inc(dve_const, 1)
            nc.vector.memset(y[0:CAP, 1, 0, :], 0.0).then_inc(dve_const, 1)
            for b, n, j, pieces in slots_of_all():
                if (b, n, j) == (-1, 1, 0):
                    dve.wait_ge(nA_exp, 1)
                    nc.vector.tensor_scalar(nA[:, :, :], nA[:, :, :], -1.0, None, ALU.mult).then_inc(nA_ready, 1)
                    dve.wait_ge(pool_const, 7)
                u = unit(b, n, j)
                if 0 <= u < 4 * N * B:
                    scan(u)
                if 0 <= u - 4 < 4 * N * B:
                    add_y(u - 4)
                for piece, m, c in pieces:
                    (front if piece == "front" else post)(m, j, c)
            for k in range(2):
                nc.vector.memset(xgT[k][:, :, CAP:CAPW], 0.0).then_inc(pad_ready, 1)

            def hide(q, r):
                dve.wait_ge(silu_ready, q * 4 + (r + 1))
                dve.wait_ge(y_ready, q * 4 + (r + 1))
                nc.vector.tensor_tensor(hid[r % 2][:, :, :].rearrange("p a c -> p (a c)"), sg[r % 2][:, :, :].rearrange("p a c -> p (a c)"),
                                        ps_gu[r % 2][:, IT * CAPW:2 * IT * CAPW], ALU.mult).then_inc(hid_ready, 1)

            dve.sem_inc(hid_ready, 2)
            with dve.Fori(0, E // 4) as q:
                for r in range(4):
                    hide(q, r)

            for b in range(B + 1):
                if b < B:
                    dve.wait_ge(fin_loaded[b], 16)
                    for tt in range(TT):
                        variance("sum", b, tt, fin[b][:, tt, :])
                for c in ([b - 2] if b >= 2 else []) + ([B - 1] if b == B else []):
                    for tt in range(2):
                        dve.wait_ge(fin_normed, 4 * c + tt + 1)
                        nc.vector.tensor_tensor(fin[c][:, tt, :], fin[c][:, tt, :], xall[:, c, tt], ALU.add).then_inc(fin_ready[c], 1)

        @block.gpsimd
        def _(pool):
            steps = [0]

            def then(ins):
                steps[0] += 1
                ins.then_inc(pool_seq, 1)
                pool.wait_ge(pool_seq, steps[0])

            def root(what, b):
                place = norm_place(what, b)
                pool.wait_ge(var_ready, NORM[what, b] + 1)
                then(nc.gpsimd.tensor_scalar(vpe[:, place, :], mv[:, place, :, 1], EPS, None, ALU.add))
                then(nc.gpsimd.tensor_tensor(rstd[:, place, :], vpe[:, place, :], mhalf[:, :], ALU.pow))
                then(nc.gpsimd.tensor_tensor(vpe[:, place, :], mv[:, place, :, 0], rstd[:, place, :], ALU.mult))
                nc.gpsimd.tensor_scalar(shift[:, place, :], vpe[:, place, :], -1.0, None, ALU.mult).then_inc(rstd_ready, 1)

            def times_b(u):
                s, dt = divmod(u, 4)
                b, n = divmod(s, N)
                if n == 0:
                    pool.wait_ge(dxd_ready, 4 * b + dt + 1)
                if dt == 0:
                    pool.wait_ge(b_spread[s % BC_RING], 16 * (s // BC_RING + 1))
                if s >= 2:
                    pool.wait_ge(h_ready, u - 7)
                nc.gpsimd.tensor_tensor(dbx[:, s % 2, dt, :], dxd[b % 2][:, dt, :], bcb[:, s % BC_RING], ALU.mult).then_inc(dbx_ready, 1)

            def front(n, j, b):
                if b == 0 and n < B and j == 3:
                    root("x", n)
                if n == 8 and b > 0:
                    pool.wait_ge(ln_ready, 4 * b + j + 1)
                    nc.gpsimd.tensor_tensor(soft[:, j], soft[:, j], onep[:, j], ALU.subtract).then_inc(log1p_ready, 1)
                if n == 10 and b > 0:
                    pool.wait_ge(delta_ready, 4 * b + j + 1)
                    nc.gpsimd.tensor_tensor(dxd[b % 2][:, j, :], delta[b % 2][:, j, :], xnT[b % 2][:, j, :], ALU.mult).then_inc(dxd_ready, 1)

            def post(n, j, b):
                if (n, j) == (1, 3):
                    root("y", b)
                if (n, j) == (3, 3):
                    root("x1", b)
                if n >= 12 and j % 2 == 0:
                    k, i = b % 2, 2 * (n - 12) + j // 2
                    if i == 0:
                        pool.wait_ge(dest_ready, b + 1)
                        if b == 0:
                            pool.wait_ge(filled, 48)
                    nc.gpsimd.indirect_dma_start(
                        out=slot_table, out_offset=bass.IndirectOffsetOnAxis(ap=desti[:, k, i:i + 1].bitcast(U32), axis=0),
                        in_=entry[:, k, i // K, i % K, :], in_offset=None, bounds_check=SLOTS - 1,
                        oob_is_err=False).then_inc(slots_written[k], 16)

            nc.gpsimd.memset(ident[:, :], 0.0).then_inc(pool_const, 1)
            pool.wait_ge(pool_const, 1)
            nc.gpsimd.affine_select(out=ident[:, :], in_=ident[:, :], compare_op=ALU.not_equal, fill=1.0, base=0,
                                    pattern=[[-1, P]], channel_multiplier=1).then_inc(pool_const, 1)
            nc.gpsimd.memset(slots[:, :, :], 0).then_inc(pool_const, 1)
            pool.wait_ge(pool_const, 3)
            nc.gpsimd.iota(slots[:, :, 0], [[0, E]], base=T, channel_multiplier=1).then_inc(pool_const, 1)
            nc.gpsimd.iota(tok[:, :], [[P, B * TT]], base=0, channel_multiplier=1).then_inc(pool_const, 1)
            nc.gpsimd.iota(iota_e[:, :], [[1, E]], base=0, channel_multiplier=0, allow_small_or_imprecise_dtypes=True).then_inc(pool_const, 1)
            nc.gpsimd.memset(mhalf[:, :], -0.5).then_inc(pool_const, 1)
            pool.wait_ge(pool_const, 7)
            for b, n, j, pieces in slots_of_all():
                u = unit(b, n, j) + 4
                if b < B and 0 <= u < 4 * N * B:
                    times_b(u)
                for piece, m, c in pieces:
                    (front if piece == "front" else post)(m, j, c)

            def gather(e):
                if e >= 4:
                    pool.wait_ge(xg_turned, e - 3)
                nc.gpsimd.indirect_dma_start(
                    out=xg[e % 4][0:CAP, :], out_offset=None, in_=x2_rows,
                    in_offset=bass.IndirectOffsetOnAxis(ap=slots[:, e, 0:1].bitcast(U32), axis=0),
                    bounds_check=T + CAP - 1, oob_is_err=False).then_inc(gathered[e % 4], 16)

            def scatter_add(e):
                pool.wait_ge(ye_ready, e + 3)
                if e >= 1:
                    pool.wait_ge(added, e * 16)
                nc.gpsimd.indirect_dma_start(
                    out=ffn_rows, in_=ye[e % 2][0:CAP, :], in_offset=None,
                    out_offset=bass.IndirectOffsetOnAxis(ap=slots[:, e, 0:1].bitcast(U32), axis=0),
                    bounds_check=T + CAP - 1, oob_is_err=True, compute_op=ALU.add).then_inc(added, 16)

            pool.wait_ge(slots_loaded, 16)
            pool.wait_ge(x2_stored, 16 * B)
            for e in range(4):
                gather(e)
            for k in range(2):
                pool.wait_ge(shared_stored[k], 16 * TT * B // 2)
            for e in range(E):
                if e + 4 < E:
                    gather(e + 4)
                scatter_add(e)

            for b in range(B + 1):
                if b < B:
                    root("sum", b)
                if b > 0:
                    for tt in range(2, TT):
                        pool.wait_ge(fin_normed, 4 * (b - 1) + tt + 1)
                        nc.gpsimd.tensor_tensor(fin[b - 1][:, tt, :], fin[b - 1][:, tt, :], xall[:, b - 1, tt], ALU.add).then_inc(fin_ready[b - 1], 1)


def kernel(L0_attn_x, L0_attn_W_xproj, L0_attn_W_dt, L0_attn_b_dt, L0_attn_A_log, L0_attn_D_param, L0_ffn_router_w,
           L0_ffn_e_bias, L0_ffn_W_gate, L0_ffn_W_up, L0_ffn_W_down, L0_ffn_shared_gate, L0_ffn_shared_up, L0_ffn_shared_down):
    import numpy as np
    import concourse.bacc as bacc
    from concourse import mybir as mb
    from concourse.bass_utils import run_bass_kernel_spmd

    def by_partition(w):
        w = np.asarray(w)
        e, rows, cols = w.shape
        return w.reshape(e, rows // 128, 128, cols).transpose(0, 2, 1, 3).reshape(e, 128, -1)

    arrays = {
        "x": np.asarray(L0_attn_x),
        "wxT": np.asarray(L0_attn_W_xproj).T,
        "wdT": np.asarray(L0_attn_W_dt).T,
        "b_dt": np.asarray(L0_attn_b_dt).reshape(DT, P).T,
        "A_log": np.asarray(L0_attn_A_log),
        "Dp": np.asarray(L0_attn_D_param).reshape(DT, P).T,
        "rwT": np.asarray(L0_ffn_router_w).T,
        "e_bias": np.asarray(L0_ffn_e_bias),
        "wexp": np.concatenate([by_partition(L0_ffn_W_gate), by_partition(L0_ffn_W_up), by_partition(L0_ffn_W_down)], axis=2),
        "sgT": np.asarray(L0_ffn_shared_gate).T,
        "suT": np.asarray(L0_ffn_shared_up).T,
        "sdT": np.asarray(L0_ffn_shared_down).T,
    }
    nc = bacc.Bacc("TRN2", target_bir_lowering=False, num_devices=1)
    in_map, args = {}, {}
    for name, a in arrays.items():
        a = np.ascontiguousarray(a)
        in_map[f"in_{name}"] = a
        args[name] = nc.dram_tensor(f"in_{name}", a.shape, mb.dt.from_np(a.dtype), kind="ExternalInput").ap()
    args["out"] = nc.dram_tensor("out_0", (B, L, D), F32, kind="ExternalOutput").ap()
    sandwich(nc, **args)
    r = run_bass_kernel_spmd(nc, [in_map], core_ids=[0])
    return r.results[0]["out_0"]
```

```python
from contextlib import ExitStack

import concourse.bass as bass
from concourse import mybir

F32 = mybir.dt.float32
I32 = mybir.dt.int32
U32 = mybir.dt.uint32
ACT = mybir.ActivationFunctionType
ALU = mybir.AluOpType
AX_X = mybir.AxisListType.X

P = 128
B, L, D = 4, 512, 512
T = B * L
TT = L // P
DT = D // P
N = 16
R = 64
XE = R + 2 * N
E, K = 32, 4
NG, TKG = 8, 3
EG = E // NG
I = 256
IT = I // P
IS = 512
ST = IS // P
CAP = -(-T * 5 // (4 * E))
CAPW = 96
SLOTS = E * CAP
SCALE = 2.5
EPS = 1e-5
WE = DT * I * 2 + IT * D
WBUF = 4
DA_RING = 3
BC_RING = 4
POST_END = 22
Y_LAG = 5
BIG = 1.0e6


POST_WIDE = {8: ("lg", 0), **{10 + 2 * i: ("g", i) for i in range(ST)}, **{11 + 2 * i: ("u", i) for i in range(ST)},
             **{18 + i: ("dn", i) for i in range(TT)}}
XDBL = {(2, 1): 0, (2, 3): 1, (3, 1): 2, (3, 3): 3}
FRONT_DRAW = 4
POST_LIGHT = {**{(7, j): ("x2T", j) for j in range(4)}, (9, 0): ("sc", 0), (11, 1): ("mT", 0), (12, 0): ("pos", 0)}
LAST_LIGHT = {**{(7, j): ("x2T", j) for j in range(4)}, (9, 0): ("sc", 0), (13, 1): ("mT", 0), (14, 1): ("pos", 0)}
FRONT_LIGHT = {**{(1, j): ("xnT", j) for j in range(4)}, **{(5, j): ("yi", j) for j in range(4)}, (6, 0): ("bc", 0)}


def beside(n, b):
    return ([("post", n + N, b - 2)] if b >= 2 and n + N < POST_END else []) + \
           ([("post", n, b - 1)] if b >= 1 else []) + ([("front", n, b + 1)] if b + 1 < B else [])


def slots_of_all():
    for n in range(N):
        for j in range(4):
            yield -1, n, j, [("front", n, 0)]
    for b in range(B):
        for n in range(N):
            for j in range(4):
                yield b, n, j, beside(n, b)
    for n in range(POST_END):
        for j in range(4):
            yield B, n, j, ([("post", n + N, B - 2)] if n + N < POST_END else []) + [("post", n, B - 1)]


def light_of(piece, n, j, b):
    table = FRONT_LIGHT if piece == "front" else LAST_LIGHT if b == B - 1 else POST_LIGHT
    return table.get((n, j))


def bank_turns():
    users = {"wide": [], "light": [], "dA": [], "ht": []}
    for _, _, j, pieces in slots_of_all():
        for piece, n, b in pieces:
            w = POST_WIDE.get(n) if piece == "post" else None
            if piece == "front" and XDBL.get((n, j)) == 0:
                users["wide"].append(("xdbl", b, 0))
            if w and j == 0:
                users["dA" if b == B - 1 and w[0] in ("g", "u") else "wide"].append((w[0], b, w[1]))
            if piece == "front" and n == FRONT_DRAW:
                users["light" if b >= 3 else "wide"].append(("draw", b, j))
            li = light_of(piece, n, j, b)
            if li:
                idle = {("xnT", 0): "dA", ("x2T", B - 1): "dA", ("yi", 0): "ht"}
                users[idle.get((li[0], b), "light")].append((li[0], b, li[1]))
    turns = {}
    for kind, first, banks in (("wide", 0, 2), ("light", 2, 1), ("dA", 3, 3), ("ht", 6, 2)):
        turns.update({u: (first + i % banks, i // banks) for i, u in enumerate(users[kind])})
    return turns


MISC = bank_turns()


def norm_order():
    return [("x", b) for b in range(B)] + [(what, b) for b in range(B) for what in ("y", "x1")] + \
        [("sum", b) for b in range(B)]


NORM = {u: i for i, u in enumerate(norm_order())}


def norm_place(what, b):
    return {"x": b, "sum": b, "y": B, "x1": B + 1}[what]


def sandwich(nc, x, wxT, wdT, b_dt, A_log, Dp, rwT, e_bias, wexp, sgT, suT, sdT, out):
    with ExitStack() as ctx:
        def sb(name, shape, dt=F32):
            return ctx.enter_context(nc.sbuf_tensor(name, shape, dt))

        def sem(name):
            return ctx.enter_context(nc.semaphore(name))

        x2_rows = nc.dram_tensor("x2_rows", [T + CAP, D], F32).ap()
        ffn_rows = nc.dram_tensor("ffn_rows", [T + CAP, D], F32).ap()
        slot_table = nc.dram_tensor("slot_table", [SLOTS, 2], I32).ap()

        b_rows = nc.dram_tensor("b_rows", [B, N, L], F32).ap()

        arena = sb("arena", [P, WBUF * WE + 4 * D + 2 * (DT + 2 * IT) * CAPW + 2 * D])
        used = [0]

        def cut(n):
            used[0] += n
            assert used[0] <= arena.shape[1]
            return arena[:, used[0] - n:used[0]]
        delta = [cut(DT * L).rearrange("p (a l) -> p a l", a=DT) for _ in range(2)]
        xnT1 = cut(DT * L).rearrange("p (a l) -> p a l", a=DT)
        dbx = cut(2 * DT * L).rearrange("p (s a l) -> p s a l", s=2, a=DT)
        h = cut(2 * DT * L).rearrange("p (s a l) -> p s a l", s=2, a=DT)
        bcb = cut(BC_RING * L).rearrange("p (s l) -> p s l", s=BC_RING)
        wring = [arena[:, k * WE:(k + 1) * WE] for k in range(WBUF)]
        used[0] = WBUF * WE
        xg = [cut(D) for _ in range(4)]
        xgT = [cut(DT * CAPW).rearrange("p (a c) -> p a c", a=DT) for _ in range(2)]
        sg = [cut(IT * CAPW).rearrange("p (a c) -> p a c", a=IT) for _ in range(2)]
        hid = [cut(IT * CAPW).rearrange("p (a c) -> p a c", a=IT) for _ in range(2)]
        ye = [cut(D) for _ in range(2)]
        fin = [arena[:, k * TT * D:(k + 1) * TT * D].rearrange("p (a l) -> p a l", a=TT) for k in range(B)]

        xall = sb("xall", [P, B, TT, D])
        y = sb("y", [P, 2, TT, D])
        nrm = sb("nrm", [P, TT, D])
        onep = sb("onep", [P, DT, L])
        xnT = [sb("xnT0", [P, DT, L]), xnT1]
        dxd = xnT
        tr = sb("tr", [P, DT, L])
        xdbl = sb("xdbl", [XE, L])
        bct = sb("bct", [P, 2, TT, XE])
        hs = sb("hs", [P, ST, L])
        soft = hs
        shout = sb("shout", [P, 2, D])
        wx, wd, rw = sb("wx", [P, DT, XE]), sb("wd", [R, D]), sb("rw", [P, DT, E])
        wsg, wsu, wsd = sb("wsg", [P, DT, IS]), sb("wsu", [P, DT, IS]), sb("wsd", [P, ST, D])
        ebias, dcol = sb("ebias", [P, E]), sb("dcol", [P, DT])
        bdt, nA = sb("bdt", [P, DT]), sb("nA", [P, DT, N])
        ident, mhalf = sb("ident", [P, P]), sb("mhalf", [P, TT])
        iota_e, tok, ones = sb("iota_e", [P, E]), sb("tok", [P, B * TT], I32), sb("ones", [E, 1])
        stat, mv = sb("stat", [P, B + 2, TT, 6]), sb("mv", [P, B + 2, TT, 2])
        vpe, rstd = sb("vpe", [P, B + 2, TT]), sb("rstd", [P, B + 2, TT])
        shift = sb("shift", [P, B + 2, TT])
        count, score, scb = sb("count", [E, L]), sb("score", [P, TT, E]), sb("scb", [P, TT, E])
        pair, gs = sb("pair", [P, 5, TT * NG]), sb("gs", [P, TT * NG])
        top8, top8i, topf = sb("top8", [P, TT, 8]), sb("top8i", [P, TT, 8], U32), sb("topf", [P, TT, 8])
        geq, gmask = sb("geq", [P, TT, TKG, NG]), sb("gmask", [P, TT, NG])
        onehot, picked = sb("onehot", [P, TT, K, E]), sb("picked", [P, TT, K, E])
        mask, carry = sb("mask", [P, TT, E]), sb("carry", [E, 1])
        lgT = count
        wsel, wsum = sb("wsel", [P, TT, K]), sb("wsum", [P, TT])
        possel, over, dest = sb("possel", [P, TT, K]), sb("over", [P, TT, K]), sb("dest", [P, TT, K])
        desti = sb("desti", [P, 2, TT * K], I32)
        entry = sb("entry", [P, 2, TT, K, 2], I32)
        slots = sb("slots", [CAP, E, 2], I32)

        def bank(name):
            return ctx.enter_context(nc.psum_tensor(name, [P, 512], F32))[:, :]
        ps_dA = [bank(f"ps_dA{i}") for i in range(DA_RING)]
        ps_ht = [bank(f"ps_ht{i}") for i in range(2)]
        ps_misc = [bank(f"ps_misc{i}") for i in range(3)] + ps_dA + ps_ht
        ps_xg, ps_gu, ps_y = ps_dA[0:2], [ps_dA[2], ps_misc[2]], ps_ht

        x_loaded = [sem(f"x_loaded{b}") for b in range(B)]
        small_loaded, shared_loaded = sem("small_loaded"), sem("shared_loaded")
        pool_const, dve_const = sem("pool_const"), sem("dve_const")
        nA_exp, nA_ready = sem("nA_exp"), sem("nA_ready")
        dA_ready, dbx_ready = sem("dA_ready"), sem("dbx_ready")
        b_stored, b_spread = sem("b_stored"), [sem(f"b_spread{k}") for k in range(BC_RING)]
        h_ready, ht_ready, y_added = sem("h_ready"), sem("ht_ready"), sem("y_added")
        misc_full = [sem(f"misc_full{k}") for k in range(8)]
        misc_taken = [sem(f"misc_taken{k}") for k in range(8)]
        dve_seq, pool_seq = sem("dve_seq"), sem("pool_seq")
        var_ready, rstd_ready = sem("var_ready"), sem("rstd_ready")
        xn_ready, xD_ready = sem("xn_ready"), sem("xD_ready")
        abs_ready, exp_ready, onep_ready = sem("abs_ready"), sem("exp_ready"), sem("onep_ready")
        corr_ready, ln_ready = sem("corr_ready"), sem("ln_ready")
        log1p_ready, delta_ready, dxd_ready = sem("log1p_ready"), sem("delta_ready"), sem("dxd_ready")
        yn_ready, x1_ready, x2_ready = sem("yn_ready"), sem("x1_ready"), sem("x2_ready")
        x2_stored = sem("x2_stored")
        mask_ready, dest_ready = sem("mask_ready"), sem("dest_ready")
        shared_stored = [sem("shared_stored0"), sem("shared_stored1")]
        filled = sem("filled")
        slots_written = [sem("slots_written0"), sem("slots_written1")]
        slots_loaded = sem("slots_loaded")
        w_loaded = [sem(f"w_loaded{k}") for k in range(WBUF)]
        gathered = [sem(f"gathered{k}") for k in range(4)]
        xg_turned, silu_ready, pad_ready = sem("xg_turned"), sem("silu_ready"), sem("pad_ready")
        xgT_ready, gu_ready, hid_ready = sem("xgT_ready"), sem("gu_ready"), sem("hid_ready")
        y_ready, ye_ready, added = sem("y_ready"), sem("ye_ready"), sem("added")
        fin_loaded = [sem(f"fin_loaded{b}") for b in range(B)]
        fin_normed, fin_stored = sem("fin_normed"), sem("fin_stored")
        fin_ready = [sem(f"fin_ready{b}") for b in range(B)]

        def wait_full(eng, *u):
            k, turn = MISC[u]
            eng.wait_ge(misc_full[k], turn + 1)
            return ps_misc[k]

        def wait_taken(eng, *u):
            k, turn = MISC[u]
            eng.wait_ge(misc_taken[k], turn + 1)

        def taken(*u):
            return misc_taken[MISC[u][0]]

        def unit(b, n, j):
            return (b * N + n) * 4 + j

        block = ctx.enter_context(nc.Block())

        @block.sync
        def _(sp):
            xv = x.rearrange("b (t p) d -> b p t d", p=P)
            sp.dma_start(xall[:, 0], xv[0]).then_inc(x_loaded[0], 16)
            sp.dma_start(wx[:], wxT.rearrange("(t p) e -> p t e", p=P)).then_inc(small_loaded, 16)
            sp.dma_start(wd[:], wdT).then_inc(small_loaded, 16)
            sp.dma_start(bdt[:], b_dt).then_inc(small_loaded, 16)
            sp.dma_start(nA[:], A_log.rearrange("(t p) n -> p t n", p=P)).then_inc(small_loaded, 16)
            sp.dma_start(dcol[:], Dp).then_inc(small_loaded, 16)
            sp.dma_start(rw[:], rwT.rearrange("(t p) e -> p t e", p=P)).then_inc(small_loaded, 16)
            sp.dma_start(ebias[:], e_bias.partition_broadcast(P)).then_inc(small_loaded, 16)
            for b in range(1, B):
                sp.dma_start(xall[:, b], xv[b]).then_inc(x_loaded[b], 16)
            sp.dma_start(wsg[:], sgT.rearrange("(t p) i -> p t i", p=P)).then_inc(shared_loaded, 16)
            sp.dma_start(wsu[:], suT.rearrange("(t p) i -> p t i", p=P)).then_inc(shared_loaded, 16)
            sp.dma_start(wsd[:], sdT.rearrange("(t p) d -> p t d", p=P)).then_inc(shared_loaded, 16)
            sp.wait_ge(dve_const, 2)
            sp.wait_ge(pool_const, 4)
            sp.dma_start(x2_rows[T:T + CAP, :], y[0:CAP, 1, 0, :]).then_inc(filled, 16)
            sp.dma_start(ffn_rows[T:T + CAP, :], y[0:CAP, 1, 0, :]).then_inc(filled, 16)
            sp.dma_start(slot_table.rearrange("(e c) k -> c e k", c=CAP), slots[:]).then_inc(filled, 16)

            def spread(s):
                b, n = divmod(s, N)
                if n == 0:
                    sp.wait_ge(b_stored, 16 * (b + 1))
                if s >= BC_RING:
                    sp.wait_ge(dbx_ready, 4 * (s - BC_RING + 1))
                sp.dma_start(bcb[:, s % BC_RING], b_rows[b, n].partition_broadcast(P)).then_inc(b_spread[s % BC_RING], 16)

            def front(n, b):
                if n == 4:
                    wait_taken(sp, "xdbl", b, 0)
                    sp.dma_start(b_rows[b], xdbl[R:R + N, :]).then_inc(b_stored, 16)

            def post(n, b):
                if n == 7:
                    sp.wait_ge(x2_ready, 4 * (b + 1))
                    sp.dma_start(x2_rows[b * L:(b + 1) * L, :].rearrange("(t p) d -> p t d", p=P), nrm[:]).then_inc(x2_stored, 16)
                if n >= 18:
                    k = b * TT + n - 18
                    wait_taken(sp, "dn", b, n - 18)
                    sp.dma_start(ffn_rows[k * P:(k + 1) * P, :], shout[:, k % 2]).then_inc(shared_stored[k % 2], 16)

            for b, n, j, pieces in slots_of_all():
                if j != 3:
                    continue
                if b == B and 8 <= n < 8 + WBUF:
                    sp.wait_ge(y_added, 4 * N * B)
                    sp.dma_start(wring[n - 8], wexp[n - 8]).then_inc(w_loaded[n - 8], 16)
                if b == B and n == 18:
                    for k in range(2):
                        sp.wait_ge(slots_written[k], 16 * TT * K * B // 2)
                    sp.dma_start(slots[:], slot_table.rearrange("(e c) k -> c e k", c=CAP)).then_inc(slots_loaded, 16)
                for piece, m, c in pieces:
                    (front if piece == "front" else post)(m, c)
                s = b * N + n
                if 0 <= s + 3 < B * N:
                    spread(s + 3)
            with sp.Fori(1, E // WBUF) as q:
                for k in range(WBUF):
                    sp.wait_ge(y_ready, q * WBUF + (k - WBUF + 3))
                    sp.dma_start(wring[k], wexp[bass.ds(q * WBUF + k, 1)].rearrange("a p w -> (a p) w")).then_inc(w_loaded[k], 16)
            sp.wait_ge(added, 16 * E)
            for b in range(B):
                rows = ffn_rows[b * L:(b + 1) * L, :].rearrange("(t p) d -> p t d", p=P)
                sp.dma_start(fin[b], rows).then_inc(fin_loaded[b], 16)
            ov = out.rearrange("b (t p) d -> b p t d", p=P)
            for b in range(B - 1):
                sp.wait_ge(fin_ready[b], TT)
                sp.dma_start(ov[b], fin[b]).then_inc(fin_stored, 16)
            for tt in range(TT):
                sp.wait_ge(fin_ready[B - 1], tt + 1)
                sp.dma_start(ov[B - 1][:, tt], fin[B - 1][:, tt]).then_inc(fin_stored, 16)
            sp.wait_ge(fin_stored, 16 * (B - 1 + TT))

        @block.tensor
        def _(pe):
            def turn4(dst, full, src, width=P):
                for j in range(4):
                    k = src(j).shape[0]
                    last = nc.tensor.transpose(dst[0:src(j).shape[1], j * width:j * width + k], src(j), ident[0:k, 0:k])
                last.then_inc(full, 1)

            def open_bank(u):
                k, turn = MISC[u]
                if turn > 0:
                    pe.wait_ge(misc_taken[k], turn)
                return ps_misc[k], misc_full[k]

            def wide(name, b, i, j):
                ps = open_bank((name, b, i))[0] if j == 0 else ps_misc[MISC[name, b, i][0]]
                full = misc_full[MISC[name, b, i][0]]
                dst = ps[:, :]
                if name == "xdbl":
                    wait_taken(pe, "xnT", b, j)
                    dst, w, v = ps[0:XE, :], wx[:, j, :], xnT[b % 2][:, j, :]
                elif name == "lg":
                    wait_taken(pe, "x2T", b, j)
                    dst, w, v = ps[0:E, :], rw[:, j, :], tr[:, j, :]
                elif name in ("g", "u"):
                    w, v = (wsg if name == "g" else wsu)[:, j, i * P:(i + 1) * P], tr[:, j, :]
                else:
                    wait_taken(pe, "u", b, j)
                    w, v = hs[:, j, i * P:(i + 1) * P], wsd[:, j, :]
                last = nc.tensor.matmul(dst, w, v, start=(j == 0), stop=(j == 3))
                if j == 3:
                    last.then_inc(full, 1)

            def light(name, b, i):
                ps, full = open_bank((name, b, i))
                if name == "xnT":
                    pe.wait_ge(xn_ready, 4 * (b + 1))
                    turn4(ps, full, lambda tt: nrm[:, tt, i * P:(i + 1) * P])
                elif name == "yi":
                    pe.wait_ge(xD_ready, 4 * (b + 1))
                    turn4(ps, full, lambda dt: tr[:, dt, i * P:(i + 1) * P])
                elif name == "bc":
                    wait_taken(pe, "xdbl", b, 0)
                    for tt in range(TT):
                        last = nc.tensor.transpose(ps[:, tt * XE:(tt + 1) * XE], xdbl[:, tt * P:(tt + 1) * P], ident[0:XE, 0:XE])
                    last.then_inc(full, 1)
                elif name == "draw":
                    wait_taken(pe, "xdbl", b, 0)
                    nc.tensor.matmul(ps[:, :], wd[:, i * P:(i + 1) * P], xdbl[0:R, :], start=True, stop=True).then_inc(full, 1)
                elif name == "x2T":
                    pe.wait_ge(x2_ready, 4 * (b + 1))
                    turn4(ps, full, lambda tt: nrm[:, tt, i * P:(i + 1) * P])
                elif name == "sc":
                    wait_taken(pe, "lg", b, 0)
                    for tt in range(TT):
                        last = nc.tensor.transpose(ps[:, tt * E:(tt + 1) * E], lgT[:, tt * P:(tt + 1) * P], ident[0:E, 0:E])
                    last.then_inc(full, 1)
                elif name == "mT":
                    pe.wait_ge(mask_ready, b + 1)
                    for tt in range(TT):
                        last = nc.tensor.transpose(ps[0:E, tt * P:(tt + 1) * P], mask[:, tt, :], ident[:, :])
                    last.then_inc(full, 1)
                else:
                    wait_taken(pe, "mT", b, 0)
                    for tt in range(TT):
                        last = nc.tensor.transpose(ps[:, tt * E:(tt + 1) * E], count[:, tt * P:(tt + 1) * P], ident[0:E, 0:E])
                    last.then_inc(full, 1)

            def turn_h(u):
                s, tt = divmod(u, 4)
                pe.wait_ge(h_ready, 4 * (s + 1))
                if u >= 2:
                    pe.wait_ge(y_added, u - 1)
                turn4(ps_ht[u % 2], ht_ready, lambda dt: h[:, s % 2, dt, tt * P:(tt + 1) * P])

            pe.wait_ge(pool_const, 2)
            pe.wait_ge(small_loaded, 16 * 7)
            for b, n, j, pieces in slots_of_all():
                u = unit(b, n, j) - Y_LAG
                if 0 <= u < 4 * N * B:
                    turn_h(u)
                for piece, m, c in pieces:
                    if m == 10 and piece == "post" and j == 0:
                        pe.wait_ge(shared_loaded, 16 * 3)
                    li = light_of(piece, m, j, c)
                    if li:
                        light(li[0], c, li[1])
                    if piece == "front" and m == FRONT_DRAW:
                        light("draw", c, j)
                    if piece == "front" and (m, j) in XDBL:
                        wide("xdbl", c, 0, XDBL[m, j])
                    if piece == "post" and m in POST_WIDE:
                        name, i = POST_WIDE[m]
                        wide(name, c, i, j)

            def turn_xg(q, r):
                pe.wait_ge(gathered[r % 4], (q + r // 4 + 1) * 16)
                pe.wait_ge(xgT_ready, q * 4 + (r + 1))
                for k in range(DT):
                    last = nc.tensor.transpose(ps_xg[r % 2][:, k * CAP:(k + 1) * CAP],
                                               xg[r % 4][0:CAP, k * P:(k + 1) * P], ident[0:CAP, 0:CAP])
                last.then_inc(xg_turned, 1)

            def gate_up(q, r):
                w = wring[r % WBUF][:, 0:2 * DT * I].rearrange("p (m k i) -> p m k i", m=2, k=DT)
                pe.wait_ge(w_loaded[r % WBUF], (q + r // WBUF + 1) * 16)
                pe.wait_ge(xgT_ready, q * 4 + (r + 3))
                pe.wait_ge(hid_ready, q * 4 + (r + 1))
                for m in range(2):
                    for it in range(IT):
                        c = (m * IT + it) * CAPW
                        for k in range(DT):
                            last = nc.tensor.matmul(ps_gu[r % 2][:, c:c + CAPW], w[:, m, k, it * P:(it + 1) * P],
                                                    xgT[r % 2][:, k, :], start=(k == 0), stop=(k == DT - 1))
                last.then_inc(gu_ready, 1)

            def down(q, r):
                w = wring[r % WBUF][:, 2 * DT * I:].rearrange("p (k d) -> p k d", k=IT)
                pe.wait_ge(hid_ready, q * 4 + (r + 3))
                pe.wait_ge(ye_ready, q * 4 + (r + 1))
                for k in range(IT):
                    last = nc.tensor.matmul(ps_y[r % 2][0:CAP, :], hid[r % 2][:, k, 0:CAP], w[:, k, :],
                                            start=(k == 0), stop=(k == IT - 1))
                last.then_inc(y_ready, 1)

            pe.sem_inc(gu_ready, 2)
            pe.sem_inc(y_ready, 2)
            pe.wait_ge(pad_ready, 2)
            turn_xg(0, 0)
            turn_xg(0, 1)
            gate_up(0, 0)
            with pe.Fori(0, E // 4 - 1) as q:
                for r in range(4):
                    turn_xg(q, r + 2)
                    gate_up(q, r + 1)
                    down(q, r)
            for r in range(4):
                if r + 2 < 4:
                    turn_xg(E // 4 - 1, r + 2)
                if r + 1 < 4:
                    gate_up(E // 4 - 1, r + 1)
                down(E // 4 - 1, r)

        @block.scalar
        def _(act):
            def take(u, dst, src, func=ACT.Copy, **kw):
                wait_full(act, *u)
                nc.scalar.activation(dst, src, func, **kw).then_inc(taken(*u), 1)

            def ps(*u):
                return ps_misc[MISC[u][0]]

            def exp_dA(u):
                (b, n), dt = divmod(u // 4, N), u % 4
                if n == 0:
                    act.wait_ge(delta_ready, 4 * b + dt + 1)
                if u >= DA_RING:
                    act.wait_ge(h_ready, u - DA_RING + 1)
                nc.scalar.activation(ps_dA[u % DA_RING], delta[b % 2][:, dt, :], ACT.Exp, scale=nA[:, dt, n:n + 1]).then_inc(dA_ready, 1)

            def normalise(what, b, tt, rows, dst, done):
                place = norm_place(what, b)
                if tt == 0:
                    act.wait_ge(rstd_ready, NORM[what, b] + 1)
                nc.scalar.activation(dst, rows, ACT.Identity, bias=shift[:, place, tt:tt + 1], scale=rstd[:, place, tt:tt + 1]).then_inc(done, 1)

            def front(n, j, b):
                if n == 0:
                    if b >= 3 and j == 0:
                        act.wait_ge(x2_stored, 16 * (b - 2))
                    normalise("x", b, j, xall[:, b, j], nrm[:, j, :], xn_ready)
                if n == 1:
                    if b >= 2 and j == 0:
                        act.wait_ge(dbx_ready, 4 * N * (b - 1))
                    take(("xnT", b, j), xnT[b % 2][:, j, :], ps("xnT", b, j))
                if n == 2:
                    if b >= 3 and j == 0:
                        wait_full(act, "u", b - 3, ST - 1)
                    wait_taken(act, "xnT", b, j)
                    nc.scalar.activation(tr[:, j, :], xnT[b % 2][:, j, :], ACT.Copy, scale=dcol[:, j:j + 1]).then_inc(xD_ready, 1)
                if (n, j) == (3, 3):
                    take(("xdbl", b, 0), xdbl[:, :], ps("xdbl", b, 0)[0:XE, :])
                if n == 5:
                    if b >= 2 and j == 0:
                        act.wait_ge(x1_ready, 4 * (b - 1))
                    if b == 1 and j == 0:
                        act.wait_ge(filled, 48)
                    take(("yi", b, j), y[:, b % 2, j], ps("yi", b, j))
                if n == 4:
                    if b >= 1 and j == 0:
                        act.wait_ge(log1p_ready, 4 * b)
                    wait_full(act, "draw", b, j)
                    nc.scalar.activation(onep[:, j], ps("draw", b, j), ACT.Abs, bias=bdt[:, j:j + 1]).then_inc(abs_ready, 1)
                    nc.scalar.activation(delta[b % 2][:, j, :], ps("draw", b, j), ACT.Relu, bias=bdt[:, j:j + 1]).then_inc(taken("draw", b, j), 1)
                if n == 7:
                    act.wait_ge(abs_ready, 4 * b + j + 1)
                    nc.scalar.activation(soft[:, j], onep[:, j], ACT.Exp, scale=-1.0).then_inc(exp_ready, 1)
                if n == 8:
                    act.wait_ge(exp_ready, 4 * b + j + 1)
                    nc.scalar.activation(onep[:, j, :], soft[:, j], ACT.Identity, bias=1.0).then_inc(onep_ready, 1)
                if n == 9 and j == 0:
                    for i in range(DT):
                        act.wait_ge(corr_ready, 4 * b + i + 1)
                        nc.scalar.activation(soft[:, i], soft[:, i], ACT.Ln, bias=1.0).then_inc(ln_ready, 1)

            def post(n, j, b):
                together = b == B - 1
                for tt in range(TT) if together and (n, j) == (2, 0) else [j] if not together and n == 3 else []:
                    normalise("y", b, tt, y[:, b % 2, tt], y[:, b % 2, tt], yn_ready)
                first = unit(0, 5, 2)
                since = unit(0, n, j) - first
                for tt in range(TT) if together and (n, j) == (5, 0) else [since] if not together and 0 <= since < TT else []:
                    if b >= 1 and tt == 0:
                        act.wait_ge(x2_stored, 16 * b)
                    normalise("x1", b, tt, xall[:, b, tt], nrm[:, tt, :], x2_ready)
                if n == 7:
                    take(("x2T", b, j), tr[:, j, :], ps("x2T", b, j))
                if (n, j) == (8, 3):
                    take(("lg", b, 0), lgT[:, :], ps("lg", b, 0)[0:E, :])
                if (n, j) == (9, 0):
                    take(("sc", b, 0), score[:, :, :].rearrange("p a e -> p (a e)"), ps("sc", b, 0)[:, 0:TT * E],
                         ACT.Exp, scale=-1.0)
                if n in (11, 13, 15, 17) and j == 0:
                    i = (n - 11) // 2
                    if b + 2 < B:
                        act.wait_ge(delta_ready, 4 * (b + 2) + i + 1)
                    take(("g", b, i), hs[:, i], ps("g", b, i), ACT.Silu)
                if n >= 18 and j == 3:
                    i = n - 18
                    k = b * TT + i
                    if k >= 2:
                        act.wait_ge(shared_stored[k % 2], 16 * (k // 2))
                    take(("dn", b, i), shout[:, k % 2], ps("dn", b, i))

            act.wait_ge(small_loaded, 16 * 7)
            nc.scalar.activation(nA[:, :, :], nA[:, :, :], ACT.Exp).then_inc(nA_exp, 1)
            for b, n, j, pieces in slots_of_all():
                u = unit(b, n, j) + DA_RING - 1
                if u >= 0 and b < B and u < 4 * N * B:
                    if u == 0:
                        act.wait_ge(nA_ready, 1)
                    exp_dA(u)
                for piece, m, c in pieces:
                    (front if piece == "front" else post)(m, j, c)

            def take_xgT(q, r):
                act.wait_ge(xg_turned, q * 4 + (r + 1))
                act.wait_ge(gu_ready, q * 4 + (r + 1))
                nc.scalar.activation(xgT[r % 2][:, :, 0:CAP], ps_xg[r % 2][:, 0:DT * CAP].rearrange("p (k c) -> p k c", k=DT),
                                     ACT.Copy).then_inc(xgT_ready, 1)

            def silu(q, r):
                act.wait_ge(gu_ready, q * 4 + (r + 3))
                act.wait_ge(hid_ready, q * 4 + (r + 1))
                nc.scalar.activation(sg[r % 2][:, :, :].rearrange("p a c -> p (a c)"), ps_gu[r % 2][:, 0:IT * CAPW], ACT.Silu).then_inc(silu_ready, 1)

            def weigh(q, r, first=False):
                e = q * 4 + r
                act.wait_ge(y_ready, q * 4 + (r + 3))
                if not first or r >= 2:
                    act.wait_ge(added, (q * 4 + (r - 1)) * 16)
                nc.scalar.activation(ye[r % 2][0:CAP, :], ps_y[r % 2][0:CAP, :], ACT.Copy,
                                     scale=slots[:, bass.ds(e, 1), 1:2].rearrange("c e k -> c (e k)").bitcast(F32)).then_inc(ye_ready, 1)

            act.sem_inc(xgT_ready, 2)
            act.sem_inc(ye_ready, 2)
            act.wait_ge(pad_ready, 2)
            act.wait_ge(slots_loaded, 16)
            take_xgT(0, 0)
            take_xgT(0, 1)
            silu(0, 0)
            for r in range(4):
                take_xgT(0, r + 2)
                silu(0, r + 1)
                weigh(0, r, first=True)
            with act.Fori(1, E // 4 - 1) as q:
                for r in range(4):
                    take_xgT(q, r + 2)
                    silu(q, r + 1)
                    weigh(q, r)
            for r in range(4):
                if r + 2 < 4:
                    take_xgT(E // 4 - 1, r + 2)
                if r + 1 < 4:
                    silu(E // 4 - 1, r + 1)
                weigh(E // 4 - 1, r)

            for b in range(B):
                for tt in range(TT):
                    normalise("sum", b, tt, fin[b][:, tt, :], fin[b][:, tt, :], fin_normed)

        @block.vector
        def _(dve):
            steps = [0]

            def step(ins):
                steps[0] += 1
                ins.then_inc(dve_seq, 1)

            def then(ins):
                step(ins)
                dve.wait_ge(dve_seq, steps[0])

            def variance(what, b, tt, rows):
                place = norm_place(what, b)
                last = nc.vector.bn_stats(stat[:, place, tt, :], rows)
                if tt == TT - 1:
                    then(last)
                    for t in range(TT):
                        last = nc.vector.bn_aggr(mv[:, place, t, :], stat[:, place, t, :])
                    last.then_inc(var_ready, 1)

            def scan(u):
                s, dt = divmod(u, 4)
                dve.wait_ge(dA_ready, u + 1)
                dve.wait_ge(dbx_ready, u + 1)
                if s >= 2:
                    dve.wait_ge(ht_ready, 4 * (s - 1))
                nc.vector.tensor_tensor_scan(h[:, s % 2, dt], ps_dA[u % DA_RING], dbx[:, s % 2, dt, :], 0.0,
                                             ALU.mult, ALU.add).then_inc(h_ready, 1)

            def add_y(u):
                (b, n), tt = divmod(u // 4, N), u % 4
                dve.wait_ge(ht_ready, u + 1)
                if n == 0:
                    wait_taken(dve, "yi", b, tt)
                else:
                    dve.wait_ge(y_added, u - 3)
                nc.vector.scalar_tensor_tensor(out=y[:, b % 2, tt], in0=ps_ht[u % 2][:, :],
                                               scalar=bct[:, b % 2, tt, R + N + n:R + N + n + 1], in1=y[:, b % 2, tt],
                                               op0=ALU.mult, op1=ALU.add).then_inc(y_added, 1)

            def add_delta(b, i):
                dve.wait_ge(log1p_ready, 4 * b + i + 1)
                nc.vector.tensor_tensor(delta[b % 2][:, i, :], delta[b % 2][:, i, :], soft[:, i], ALU.add).then_inc(delta_ready, 1)

            def front(n, j, b):
                if b == 0 and n < B:
                    if j == 0:
                        dve.wait_ge(x_loaded[n], 16)
                    variance("x", n, j, xall[:, n, j, :])
                if (n, j) == (6, 1):
                    ps = wait_full(dve, "bc", b, 0)
                    nc.vector.tensor_copy(bct[:, b % 2].rearrange("p a e -> p (a e)"), ps[:, 0:TT * XE]).then_inc(taken("bc", b, 0), 1)
                if n == 8:
                    dve.wait_ge(onep_ready, 4 * b + j + 1)
                    nc.vector.scalar_tensor_tensor(out=onep[:, j], in0=onep[:, j], scalar=1.0, in1=soft[:, j],
                                                   op0=ALU.subtract, op1=ALU.subtract).then_inc(corr_ready, 1)
                if n == 9 and b == 0:
                    dve.wait_ge(ln_ready, j + 1)
                    nc.vector.tensor_tensor(soft[:, j], soft[:, j], onep[:, j], ALU.subtract).then_inc(log1p_ready, 1)
                    add_delta(b, j)
                    dve.wait_ge(delta_ready, j + 1)
                    nc.vector.tensor_tensor(dxd[b % 2][:, j, :], delta[b % 2][:, j, :], xnT[b % 2][:, j, :], ALU.mult).then_inc(dxd_ready, 1)
                if n == 10 and b > 0:
                    add_delta(b, j)

            def hidden_up(b, i):
                wait_taken(dve, "g", b, i)
                ps = wait_full(dve, "u", b, i)
                nc.vector.tensor_tensor(hs[:, i], hs[:, i], ps[:, :], ALU.mult).then_inc(taken("u", b, i), 1)

            def best8(part, rows):
                if part == 2:
                    step(nc.vector.tensor_copy(topf[:, :, :], top8i[:, :, :]))
                    return
                for tt in range(TT):
                    last = nc.vector.max(top8[:, tt, :], rows(tt)) if part == 0 else \
                        nc.vector.max_index(top8i[:, tt, :], top8[:, tt, :], rows(tt))
                step(last)

            def tile32(a):
                return a[:, :, :].rearrange("p a (g m) -> p (a g) m", m=EG)

            def choose(b, stage):
                v = tile32(scb)
                if stage == 0:
                    wait_taken(dve, "sc", b, 0)
                elif stage < 23:
                    dve.wait_ge(dve_seq, steps[0])
                if stage == 0:
                    step(nc.vector.tensor_scalar(score[:, :, :], score[:, :, :], 1.0, None, ALU.add))
                elif stage == 1:
                    step(nc.vector.reciprocal(score[:, :, :], score[:, :, :]))
                elif stage == 2:
                    step(nc.vector.tensor_tensor(scb[:, :, :], score[:, :, :], ebias[:, :].unsqueeze(1).to_broadcast([P, TT, E]), ALU.add))
                elif stage == 3:
                    nc.vector.tensor_tensor(pair[:, 0], v[:, :, 0], v[:, :, 1], ALU.max)
                    nc.vector.tensor_tensor(pair[:, 1], v[:, :, 2], v[:, :, 3], ALU.max)
                    nc.vector.tensor_tensor(pair[:, 2], v[:, :, 0], v[:, :, 1], ALU.add)
                    step(nc.vector.tensor_tensor(pair[:, 3], v[:, :, 2], v[:, :, 3], ALU.add))
                elif stage == 4:
                    nc.vector.tensor_tensor(pair[:, 4], pair[:, 0], pair[:, 1], ALU.add)
                    step(nc.vector.tensor_tensor(gs[:, :], pair[:, 2], pair[:, 3], ALU.max))
                elif stage == 5:
                    step(nc.vector.tensor_tensor(gs[:, :], gs[:, :], pair[:, 4], ALU.max))
                elif stage == 6:
                    best8(0, lambda tt: gs[:, tt * NG:(tt + 1) * NG])
                elif stage == 7:
                    best8(1, lambda tt: gs[:, tt * NG:(tt + 1) * NG])
                elif stage == 8:
                    best8(2, lambda tt: gs[:, tt * NG:(tt + 1) * NG])
                elif stage == 9:
                    step(nc.vector.tensor_tensor(geq[:, :, :, :], topf[:, :, 0:TKG].unsqueeze(3).to_broadcast([P, TT, TKG, NG]),
                        iota_e[:, 0:NG].unsqueeze(1).unsqueeze(1).to_broadcast([P, TT, TKG, NG]), ALU.is_equal))
                elif stage == 10:
                    step(nc.vector.tensor_reduce(gmask[:, :, :], geq[:, :, :, :].rearrange("p a k g -> p a g k"), AX_X, ALU.add))
                elif stage == 11:
                    step(nc.vector.tensor_tensor(v, v, gmask[:, :, :].rearrange("p a g -> p (a g)").unsqueeze(2).to_broadcast([P, TT * NG, EG]), ALU.mult))
                elif stage == 12:
                    step(nc.vector.tensor_scalar(scb[:, :, :], scb[:, :, :], 0.0, None, ALU.add))
                elif stage == 13:
                    best8(0, lambda tt: scb[:, tt, :])
                elif stage == 14:
                    best8(1, lambda tt: scb[:, tt, :])
                elif stage == 15:
                    best8(2, lambda tt: scb[:, tt, :])
                elif stage == 16:
                    step(nc.vector.tensor_tensor(onehot[:, :, :, :], topf[:, :, 0:K].unsqueeze(3).to_broadcast([P, TT, K, E]),
                        iota_e[:, :].unsqueeze(1).unsqueeze(1).to_broadcast([P, TT, K, E]), ALU.is_equal))
                elif stage == 17:
                    nc.vector.tensor_reduce(mask[:, :, :], onehot[:, :, :, :].rearrange("p a k e -> p a e k"), AX_X, ALU.add).then_inc(mask_ready, 1)
                    step(nc.vector.tensor_tensor(picked[:, :, :, :], onehot[:, :, :, :], score[:, :, :].unsqueeze(2).to_broadcast([P, TT, K, E]), ALU.mult))
                elif stage == 18:
                    step(nc.vector.tensor_reduce(wsel[:, :, :], picked[:, :, :, :], AX_X, ALU.add))
                elif stage == 19:
                    step(nc.vector.tensor_reduce(wsum[:, :], wsel[:, :, :], AX_X, ALU.add))
                elif stage == 20:
                    step(nc.vector.tensor_scalar(wsum[:, :], wsum[:, :], 1e-20, None, ALU.add))
                elif stage == 21:
                    step(nc.vector.reciprocal(wsum[:, :], wsum[:, :]))
                elif stage == 22:
                    step(nc.vector.tensor_tensor(wsel[:, :, :], wsel[:, :, :], wsum[:, :].unsqueeze(2).to_broadcast([P, TT, K]), ALU.mult))

            def queue(b):
                ps = wait_full(dve, "mT", b, 0)
                nc.vector.tensor_tensor_scan(count[:, :], ones[:, :].to_broadcast([E, L]), ps[0:E, :], carry[:, 0:1], ALU.mult, ALU.add).then_inc(taken("mT", b, 0), 1)
                wait_taken(dve, "mT", b, 0)
                then(nc.vector.tensor_copy(carry[:, :], count[:, L - 1:L]))

            def destine(b):
                k = b % 2
                ps = wait_full(dve, "pos", b, 0)
                nc.vector.tensor_tensor(picked[:, :, :, :], onehot[:, :, :, :],
                                        ps[:, 0:TT * E].rearrange("p (a e) -> p a e", a=TT).unsqueeze(2).to_broadcast([P, TT, K, E]),
                                        ALU.mult).then_inc(taken("pos", b, 0), 1)
                wait_taken(dve, "pos", b, 0)
                then(nc.vector.tensor_reduce(possel[:, :, :], picked[:, :, :, :], AX_X, ALU.add))
                then(nc.vector.tensor_scalar(over[:, :, :], possel[:, :, :], float(CAP), BIG, ALU.is_gt, ALU.mult))
                then(nc.vector.tensor_tensor(over[:, :, :], over[:, :, :], possel[:, :, :], ALU.add))
                then(nc.vector.scalar_tensor_tensor(out=dest[:, :, :], in0=topf[:, :, 0:K], scalar=float(CAP), in1=over[:, :, :],
                                                    op0=ALU.mult, op1=ALU.add))
                if b >= 2:
                    dve.wait_ge(slots_written[k], 16 * TT * K * (b // 2))
                nc.vector.tensor_scalar(desti[:, k, :], dest[:, :, :].rearrange("p a k -> p (a k)"), -1.0, None, ALU.add)
                nc.vector.tensor_scalar(entry[:, k, :, :, 1].bitcast(F32), wsel[:, :, :], SCALE, None, ALU.mult)
                nc.vector.tensor_copy(entry[:, k, :, :, 0], tok[:, b * TT:(b + 1) * TT].unsqueeze(2).to_broadcast([P, TT, K])).then_inc(dest_ready, 1)

            def add_x(b, tt):
                dve.wait_ge(yn_ready, 4 * b + tt + 1)
                nc.vector.tensor_tensor(xall[:, b, tt], xall[:, b, tt], y[:, b % 2, tt], ALU.add).then_inc(x1_ready, 1)

            def at(n, j):
                return (n - 9) * 4 + j

            def post(n, j, b):
                tt = 4 * n + j - (Y_LAG - 4 if b == B - 1 else 4)
                if 0 <= tt < TT:
                    dve.wait_ge(y_added, 4 * N * (b + 1) - 3 + tt)
                    variance("y", b, tt, y[:, b % 2, tt])
                add, of = {(3, 1): (0, None), (3, 2): (1, 0), (3, 3): (2, 1), (4, 0): (3, None), (4, 1): (None, 2),
                           (4, 2): (None, 3)}.get((n, j), (None, None))
                if add is not None:
                    add_x(b, add)
                if of is not None:
                    dve.wait_ge(x1_ready, 4 * b + of + 1)
                    variance("x1", b, of, xall[:, b, of])
                if 1 <= at(n, j) <= 8:
                    choose(b, 3 * at(n, j) - 2)
                    choose(b, 3 * at(n, j) - 1)
                if (n, j) == (11, 2):
                    queue(b)
                if (n, j) == (12, 1):
                    destine(b)
                if n in (12, 14, 16, 18) and j == 0:
                    hidden_up(b, (n - 12) // 2)

            nc.vector.memset(carry[:, :], 0.0)
            nc.vector.memset(ones[:, :], 1.0).then_inc(dve_const, 1)
            nc.vector.memset(y[0:CAP, 1, 0, :], 0.0).then_inc(dve_const, 1)
            for b, n, j, pieces in slots_of_all():
                if (b, n, j) == (-1, 1, 0):
                    dve.wait_ge(nA_exp, 1)
                    nc.vector.tensor_scalar(nA[:, :, :], nA[:, :, :], -1.0, None, ALU.mult).then_inc(nA_ready, 1)
                    dve.wait_ge(pool_const, 7)
                u = unit(b, n, j)
                if 0 <= u < 4 * N * B:
                    scan(u)
                for piece, m, c in pieces:
                    if piece == "post" and 1 <= at(m, j) <= 8:
                        choose(c, 3 * at(m, j) - 3)
                if 0 <= u - Y_LAG < 4 * N * B:
                    add_y(u - Y_LAG)
                for piece, m, c in pieces:
                    (front if piece == "front" else post)(m, j, c)
            for k in range(2):
                nc.vector.memset(xgT[k][:, :, CAP:CAPW], 0.0).then_inc(pad_ready, 1)

            def hide(q, r):
                dve.wait_ge(silu_ready, q * 4 + (r + 1))
                dve.wait_ge(y_ready, q * 4 + (r + 1))
                nc.vector.tensor_tensor(hid[r % 2][:, :, :].rearrange("p a c -> p (a c)"), sg[r % 2][:, :, :].rearrange("p a c -> p (a c)"),
                                        ps_gu[r % 2][:, IT * CAPW:2 * IT * CAPW], ALU.mult).then_inc(hid_ready, 1)

            dve.sem_inc(hid_ready, 2)
            with dve.Fori(0, E // 4) as q:
                for r in range(4):
                    hide(q, r)

            for b in range(B + 1):
                if b < B:
                    dve.wait_ge(fin_loaded[b], 16)
                    for tt in range(TT):
                        variance("sum", b, tt, fin[b][:, tt, :])
                for c in ([b - 2] if b >= 2 else []) + ([B - 1] if b == B else []):
                    for tt in range(2 if c < B - 1 else TT):
                        dve.wait_ge(fin_normed, 4 * c + tt + 1)
                        nc.vector.tensor_tensor(fin[c][:, tt, :], fin[c][:, tt, :], xall[:, c, tt], ALU.add).then_inc(fin_ready[c], 1)

        @block.gpsimd
        def _(pool):
            steps = [0]

            def then(ins):
                steps[0] += 1
                ins.then_inc(pool_seq, 1)
                pool.wait_ge(pool_seq, steps[0])

            def root(what, b):
                place = norm_place(what, b)
                pool.wait_ge(var_ready, NORM[what, b] + 1)
                then(nc.gpsimd.tensor_scalar(vpe[:, place, :], mv[:, place, :, 1], EPS, None, ALU.add))
                then(nc.gpsimd.tensor_tensor(rstd[:, place, :], vpe[:, place, :], mhalf[:, :], ALU.pow))
                then(nc.gpsimd.tensor_tensor(vpe[:, place, :], mv[:, place, :, 0], rstd[:, place, :], ALU.mult))
                nc.gpsimd.tensor_scalar(shift[:, place, :], vpe[:, place, :], -1.0, None, ALU.mult).then_inc(rstd_ready, 1)

            def times_b(u):
                s, dt = divmod(u, 4)
                b, n = divmod(s, N)
                if n == 0:
                    pool.wait_ge(dxd_ready, 4 * b + dt + 1)
                if dt == 0:
                    pool.wait_ge(b_spread[s % BC_RING], 16 * (s // BC_RING + 1))
                if s >= 2:
                    pool.wait_ge(h_ready, u - 7)
                nc.gpsimd.tensor_tensor(dbx[:, s % 2, dt, :], dxd[b % 2][:, dt, :], bcb[:, s % BC_RING], ALU.mult).then_inc(dbx_ready, 1)

            def front(n, j, b):
                if b == 0 and n < B and j == 3:
                    root("x", n)
                if n == 9 and b > 0:
                    pool.wait_ge(ln_ready, 4 * b + j + 1)
                    nc.gpsimd.tensor_tensor(soft[:, j], soft[:, j], onep[:, j], ALU.subtract).then_inc(log1p_ready, 1)
                if n == 11 and b > 0:
                    pool.wait_ge(delta_ready, 4 * b + j + 1)
                    nc.gpsimd.tensor_tensor(dxd[b % 2][:, j, :], delta[b % 2][:, j, :], xnT[b % 2][:, j, :], ALU.mult).then_inc(dxd_ready, 1)

            def post(n, j, b):
                if (n, j) == (2, 2):
                    root("y", b)
                if (n, j) == (4, 3):
                    root("x1", b)
                if n >= 14 and j % 2 == 0:
                    k, i = b % 2, 2 * (n - 14) + j // 2
                    if i == 0:
                        pool.wait_ge(dest_ready, b + 1)
                        if b == 0:
                            pool.wait_ge(filled, 48)
                    nc.gpsimd.indirect_dma_start(
                        out=slot_table, out_offset=bass.IndirectOffsetOnAxis(ap=desti[:, k, i:i + 1].bitcast(U32), axis=0),
                        in_=entry[:, k, i // K, i % K, :], in_offset=None, bounds_check=SLOTS - 1,
                        oob_is_err=False).then_inc(slots_written[k], 16)

            nc.gpsimd.memset(ident[:, :], 0.0).then_inc(pool_const, 1)
            pool.wait_ge(pool_const, 1)
            nc.gpsimd.affine_select(out=ident[:, :], in_=ident[:, :], compare_op=ALU.not_equal, fill=1.0, base=0,
                                    pattern=[[-1, P]], channel_multiplier=1).then_inc(pool_const, 1)
            nc.gpsimd.memset(slots[:, :, :], 0).then_inc(pool_const, 1)
            pool.wait_ge(pool_const, 3)
            nc.gpsimd.iota(slots[:, :, 0], [[0, E]], base=T, channel_multiplier=1).then_inc(pool_const, 1)
            nc.gpsimd.iota(tok[:, :], [[P, B * TT]], base=0, channel_multiplier=1).then_inc(pool_const, 1)
            nc.gpsimd.iota(iota_e[:, :], [[1, E]], base=0, channel_multiplier=0, allow_small_or_imprecise_dtypes=True).then_inc(pool_const, 1)
            nc.gpsimd.memset(mhalf[:, :], -0.5).then_inc(pool_const, 1)
            pool.wait_ge(pool_const, 7)
            for b, n, j, pieces in slots_of_all():
                u = unit(b, n, j) + 4
                if b < B and 0 <= u < 4 * N * B:
                    times_b(u)
                for piece, m, c in pieces:
                    (front if piece == "front" else post)(m, j, c)

            def gather(e):
                if e >= 4:
                    pool.wait_ge(xg_turned, e - 3)
                nc.gpsimd.indirect_dma_start(
                    out=xg[e % 4][0:CAP, :], out_offset=None, in_=x2_rows,
                    in_offset=bass.IndirectOffsetOnAxis(ap=slots[:, e, 0:1].bitcast(U32), axis=0),
                    bounds_check=T + CAP - 1, oob_is_err=False).then_inc(gathered[e % 4], 16)

            def scatter_add(e):
                pool.wait_ge(ye_ready, e + 3)
                if e >= 1:
                    pool.wait_ge(added, e * 16)
                nc.gpsimd.indirect_dma_start(
                    out=ffn_rows, in_=ye[e % 2][0:CAP, :], in_offset=None,
                    out_offset=bass.IndirectOffsetOnAxis(ap=slots[:, e, 0:1].bitcast(U32), axis=0),
                    bounds_check=T + CAP - 1, oob_is_err=True, compute_op=ALU.add).then_inc(added, 16)

            pool.wait_ge(slots_loaded, 16)
            pool.wait_ge(x2_stored, 16 * B)
            for e in range(4):
                gather(e)
            for k in range(2):
                pool.wait_ge(shared_stored[k], 16 * TT * B // 2)
            for e in range(E):
                if e + 4 < E:
                    gather(e + 4)
                scatter_add(e)

            def add_sum(b):
                for tt in range(2, TT):
                    pool.wait_ge(fin_normed, 4 * b + tt + 1)
                    nc.gpsimd.tensor_tensor(fin[b][:, tt, :], fin[b][:, tt, :], xall[:, b, tt], ALU.add).then_inc(fin_ready[b], 1)

            for b in range(B):
                root("sum", b)
                if 0 < b < B - 1:
                    add_sum(b - 1)
            add_sum(B - 2)


def kernel(L0_attn_x, L0_attn_W_xproj, L0_attn_W_dt, L0_attn_b_dt, L0_attn_A_log, L0_attn_D_param, L0_ffn_router_w,
           L0_ffn_e_bias, L0_ffn_W_gate, L0_ffn_W_up, L0_ffn_W_down, L0_ffn_shared_gate, L0_ffn_shared_up, L0_ffn_shared_down):
    import numpy as np
    import concourse.bacc as bacc
    from concourse import mybir as mb
    from concourse.bass_utils import run_bass_kernel_spmd

    def by_partition(w):
        w = np.asarray(w)
        e, rows, cols = w.shape
        return w.reshape(e, rows // 128, 128, cols).transpose(0, 2, 1, 3).reshape(e, 128, -1)

    arrays = {
        "x": np.asarray(L0_attn_x),
        "wxT": np.asarray(L0_attn_W_xproj).T,
        "wdT": np.asarray(L0_attn_W_dt).T,
        "b_dt": np.asarray(L0_attn_b_dt).reshape(DT, P).T,
        "A_log": np.asarray(L0_attn_A_log),
        "Dp": np.asarray(L0_attn_D_param).reshape(DT, P).T,
        "rwT": np.asarray(L0_ffn_router_w).T,
        "e_bias": np.asarray(L0_ffn_e_bias),
        "wexp": np.concatenate([by_partition(L0_ffn_W_gate), by_partition(L0_ffn_W_up), by_partition(L0_ffn_W_down)], axis=2),
        "sgT": np.asarray(L0_ffn_shared_gate).T,
        "suT": np.asarray(L0_ffn_shared_up).T,
        "sdT": np.asarray(L0_ffn_shared_down).T,
    }
    nc = bacc.Bacc("TRN2", target_bir_lowering=False, num_devices=1)
    in_map, args = {}, {}
    for name, a in arrays.items():
        a = np.ascontiguousarray(a)
        in_map[f"in_{name}"] = a
        args[name] = nc.dram_tensor(f"in_{name}", a.shape, mb.dt.from_np(a.dtype), kind="ExternalInput").ap()
    args["out"] = nc.dram_tensor("out_0", (B, L, D), F32, kind="ExternalOutput").ap()
    sandwich(nc, **args)
    r = run_bass_kernel_spmd(nc, [in_map], core_ids=[0])
    return r.results[0]["out_0"]
```
